# Optimizing a Trainium2 kernel written in Bass

```python
import numpy as np
import jax
import jax.numpy as jnp

def _softmax(x, axis=-1):
    return jax.nn.softmax(x, axis=axis)

def _gelu(x):
    return jax.nn.gelu(x, approximate=True)

def _silu(x):
    return jax.nn.silu(x)

def _sigmoid(x):
    return jax.nn.sigmoid(x)

def _layernorm(x, axis=-1, eps=1e-05):
    m = jnp.mean(x, axis=axis, keepdims=True)
    v = jnp.var(x, axis=axis, keepdims=True)
    return (x - m) / jnp.sqrt(v + eps)

def _scatter_add(tgt, idx, src, axis=0):
    return tgt.at[idx].add(src)

def _segment_sum(src, seg, n):
    return jax.ops.segment_sum(src, seg, n)
kernel_name = 'mk_macaron_d1_jaxref_r4_6ec191'

def setup_inputs(seed: int=0):
    np.random.seed(seed)
    _w = jnp.asarray

    def _L0_attn_setup():
        import jax, jax.numpy as jnp
        import numpy as np
        import math
        D_MODEL = 256
        NUM_HEADS = 16
        HEAD_DIM = D_MODEL // NUM_HEADS
        key = jax.random.key(seed)
        k_x, k_qkv, k_o = jax.random.split(key, 3)
        B, S = (2, 512)
        x = jax.random.normal(k_x, (B, S, D_MODEL), dtype=jnp.float32)
        sigma_qkv = math.sqrt(2.0 / (D_MODEL + 3 * D_MODEL))
        w_qkv = jax.random.truncated_normal(k_qkv, -3.0, 3.0, (3 * D_MODEL, D_MODEL), dtype=jnp.float32) * sigma_qkv
        sigma_o = math.sqrt(2.0 / (D_MODEL + D_MODEL))
        w_out = jax.random.truncated_normal(k_o, -3.0, 3.0, (D_MODEL, D_MODEL), dtype=jnp.float32) * sigma_o
        return {'x': x, 'w_qkv': w_qkv, 'w_out': w_out}
    _L0_attn_in = _L0_attn_setup()

    def _L0_ffn_setup():
        import jax, jax.numpy as jnp
        import numpy as np
        K = 2
        key = jax.random.key(seed)
        ks = jax.random.split(key, 9)
        B, S, D, O, E = (4, 256, 256, 256, 8)
        sc = 0.02
        return {'x': jax.random.normal(ks[0], (B, S, D), dtype=jnp.float32), 'gate_w': jax.random.normal(ks[1], (D, E), dtype=jnp.float32) * sc, 'gate_b': jax.random.normal(ks[2], (E,), dtype=jnp.float32) * sc, 'w1': jax.random.normal(ks[3], (E, D, O), dtype=jnp.float32) * sc, 'b1': jax.random.normal(ks[4], (E, O), dtype=jnp.float32) * sc, 'w2': jax.random.normal(ks[5], (E, O, O), dtype=jnp.float32) * sc, 'b2': jax.random.normal(ks[6], (E, O), dtype=jnp.float32) * sc, 'w3': jax.random.normal(ks[7], (E, O, O), dtype=jnp.float32) * sc, 'b3': jax.random.normal(ks[8], (E, O), dtype=jnp.float32) * sc}
    _L0_ffn_in = _L0_ffn_setup()
    _d = {'L0_attn_x': _L0_attn_in['x'], 'L0_attn_w_qkv': _L0_attn_in['w_qkv'], 'L0_attn_w_out': _L0_attn_in['w_out'], 'L0_ffn_gate_w': _L0_ffn_in['gate_w'], 'L0_ffn_gate_b': _L0_ffn_in['gate_b'], 'L0_ffn_w1': _L0_ffn_in['w1'], 'L0_ffn_b1': _L0_ffn_in['b1'], 'L0_ffn_w2': _L0_ffn_in['w2'], 'L0_ffn_b2': _L0_ffn_in['b2'], 'L0_ffn_w3': _L0_ffn_in['w3'], 'L0_ffn_b3': _L0_ffn_in['b3']}
    _x0 = _d['L0_attn_x']
    _d['L0_attn_x'] = jax.random.normal(jax.random.fold_in(jax.random.key(seed), 1), (1, 4096, 256), dtype=_x0.dtype)
    del _x0
    return _d

def reference(L0_attn_x, L0_attn_w_qkv, L0_attn_w_out, L0_ffn_gate_w, L0_ffn_gate_b, L0_ffn_w1, L0_ffn_b1, L0_ffn_w2, L0_ffn_b2, L0_ffn_w3, L0_ffn_b3):

    def _L0_attn_ref(x, w_qkv, w_out):
        import jax, jax.numpy as jnp
        import numpy as np
        import math
        D_MODEL = 256
        NUM_HEADS = 16
        HEAD_DIM = D_MODEL // NUM_HEADS
        B, S, _ = x.shape
        qkv = jnp.einsum('bsi,oi->bso', x, w_qkv)
        q, k, v = jnp.split(qkv, 3, axis=-1)

        def to_heads(t):
            return t.reshape(B, S, NUM_HEADS, HEAD_DIM).transpose(0, 2, 1, 3)
        q, k, v = (to_heads(q), to_heads(k), to_heads(v))
        scale = 1.0 / math.sqrt(HEAD_DIM)
        logits = jnp.einsum('bhsd,bhtd->bhst', q, k) * scale
        mask = jnp.tril(jnp.ones((S, S), dtype=bool))
        neg_inf = jnp.finfo(jnp.float32).min
        logits = jnp.where(mask, logits, neg_inf)
        probs = jax.nn.softmax(logits, axis=-1)
        probs = probs * mask.astype(probs.dtype)
        out = jnp.einsum('bhst,bhtd->bhsd', probs, v)
        out = out.transpose(0, 2, 1, 3).reshape(B, S, D_MODEL)
        return jnp.einsum('bsi,oi->bso', out, w_out)

    def _L0_ffn_ref(x, gate_w, gate_b, w1, b1, w2, b2, w3, b3):
        import jax, jax.numpy as jnp
        import numpy as np
        K = 2
        E = gate_w.shape[-1]
        logits = jnp.einsum('bsd,de->bse', x, gate_w) + gate_b
        probs = jax.nn.softmax(logits, axis=1)
        vals, idx = jax.lax.top_k(probs, K)
        h = jax.nn.relu(jnp.einsum('bsd,edo->ebso', x, w1) + b1[:, None, None, :])
        h = jax.nn.relu(jnp.einsum('ebso,eop->ebsp', h, w2) + b2[:, None, None, :])
        y = jax.nn.relu(jnp.einsum('ebso,eop->ebsp', h, w3) + b3[:, None, None, :])
        onehot = jax.nn.one_hot(idx, E, dtype=x.dtype)
        w_tok = jnp.einsum('bske,bsk->bse', onehot, vals)
        ind = onehot.max(axis=2)
        v = jnp.einsum('ebso,bse->eo', y, w_tok)
        out = jnp.einsum('bse,eo->bso', ind, v)
        return out
    x = L0_attn_x
    x = x + 0.5 * _L0_ffn_ref(_layernorm(x, axis=-1), L0_ffn_gate_w, L0_ffn_gate_b, L0_ffn_w1, L0_ffn_b1, L0_ffn_w2, L0_ffn_b2, L0_ffn_w3, L0_ffn_b3)
    x = x + _L0_attn_ref(_layernorm(x, axis=-1), L0_attn_w_qkv, L0_attn_w_out)
    x = x + 0.5 * _L0_ffn_ref(_layernorm(x, axis=-1), L0_ffn_gate_w, L0_ffn_gate_b, L0_ffn_w1, L0_ffn_b1, L0_ffn_w2, L0_ffn_b2, L0_ffn_w3, L0_ffn_b3)
    return x

_drawn_inputs = setup_inputs


def setup_inputs(seed=0):
    import zlib

    import numpy as np

    out = dict(_drawn_inputs(seed))
    spreads = {}
    factors = {'L0_ffn_gate_w': 8.0,
     'L0_ffn_gate_b': 8.0,
     'L0_ffn_w1': 8.0,
     'L0_ffn_b1': 8.0,
     'L0_ffn_w2': 8.0,
     'L0_ffn_b2': 8.0,
     'L0_ffn_w3': 8.0,
     'L0_ffn_b3': 8.0}
    for name, (base, spread) in spreads.items():
        noise = np.random.default_rng([zlib.crc32(name.encode()), seed]).standard_normal(out[name].shape)
        drawn = base * np.exp(spread * noise) if base else spread * noise
        out[name] = jnp.asarray(drawn.astype(out[name].dtype))
    for name, factor in factors.items():
        out[name] = (out[name] * factor).astype(out[name].dtype)
    return out
```

```python
from contextlib import ExitStack

import concourse.bass as bass
from concourse import mybir

F32 = mybir.dt.float32
BF16 = mybir.dt.bfloat16
U32 = mybir.dt.uint32
I32 = mybir.dt.int32
ALU = mybir.AluOpType
ACT = mybir.ActivationFunctionType
AX_X = mybir.AxisListType.X
REDUCE = bass.bass_isa.ReduceOp

P = 128
S = 4096
D = 256
NT = S // P
KD = D // P
H = 16
HD = D // H
E = 8
LAYERS = 3
TOP = 2
EPS = 1e-5
NEG = -3.0e38

TILE = 256
TS = TILE // P
N_TILES = (TOP * S + E * (TILE - 1)) // TILE
ROW = D + E
WROW = KD * D + KD

QB = 512
NJ = S // QB
TPJ = QB // P
PARTS = ((0, 0), (0, 1), (0, 2), (1, 0), (1, 1), (2, 0))
QK_ROWS = len(PARTS) * HD
M_PARTS = 2
VW = HD + 1
S_BANKS = (0, 1, 2)
A_BANKS = (3, 4)
ACC_BANK, M_BANK, O_BANK = 5, 6, 7
WORK = 10368
P_RING = 8
LEAD = 44


class Counter:

    def __init__(self, sem):
        self.sem, self.count = sem, 0


class Queues:

    def __init__(self, nc, ctx):
        self.nc, self.ctx = nc, ctx
        self.lists = {name: [] for name in ("tensor", "vector", "scalar", "gpsimd", "sync")}

    def counter(self, name):
        return Counter(self.ctx.enter_context(self.nc.semaphore(name)))

    def put(self, engine, emit, waits=(), counter=None, amount=1):
        mark = None
        if counter is not None:
            counter.count += amount
            mark = (counter, counter.count)
        self.lists[engine].append((tuple(w for w in waits if w is not None), emit, counter, amount))
        return mark

    def dma(self, engine, out, in_, waits, counter):
        return self.put(engine, lambda e: e.dma_start(out, in_), waits, counter, 16)

    def run(self, engine, eng):
        reached = {}
        for waits, emit, counter, amount in self.lists[engine]:
            for s, value in waits:
                if reached.get(s, 0) < value:
                    eng.wait_ge(s.sem, value)
                    reached[s] = value
            ins = emit(eng)
            if counter is not None:
                ins.then_inc(counter.sem, amount)


def macaron_block(nc, x_in, w_qkv_t, w_out_t, gate_w, gate_b, w1, w2, w3, bias_cols, out):
    with ExitStack() as ctx:
        q = Queues(nc, ctx)
        sig, put, dma = q.counter, q.put, q.dma

        def sb(name, shape, dt=F32):
            return ctx.enter_context(nc.sbuf_tensor(name, shape, dt))

        x_res = sb("x_res", [P, NT, D])
        rows = sb("rows", [P, NT, ROW])
        feat = sb("feat", [P, KD, S])
        phase = sb("phase", [P, E * LAYERS * WROW])
        ident = sb("ident", [P, P])
        ident_bf = sb("ident_bf", [P, P], BF16)
        stats = sb("stats", [P, NT, 6])
        mean_var = sb("mean_var", [P, NT, 2])
        rstd = sb("rstd", [P, 2, NT])
        w_qkv_sb = sb("w_qkv_sb", [P, KD, 3 * D])
        w_out_sb = sb("w_out_sb", [P, KD, D])
        zero_row = sb("zero_row", [P, ROW])
        bank = [ctx.enter_context(nc.psum_tensor(f"bank{i}", [P, 512], F32)) for i in range(8)]
        free = {i: () for i in range(8)}

        slots = [nc.dram_tensor(f"slots{f}", (N_TILES * TILE, ROW), F32).ap() for f in range(2)]
        parts_dram = nc.dram_tensor("qk_parts", (2, 3, D, S), BF16).ap()

        s_const = sig("constants")

        def const(emit):
            last = (s_const, s_const.count) if s_const.count else None
            return put("gpsimd", emit, [last], s_const)

        def diagonal(t, n=P):
            const(lambda e: e.memset(t, 0.0))
            const(lambda e: e.affine_select(out=t, in_=t, compare_op=ALU.not_equal, fill=1.0, base=0,
                                            pattern=[[-1, n]], channel_multiplier=1))

        diagonal(ident[:, :])
        diagonal(ident_bf[:, :])
        const(lambda e: e.memset(zero_row[:, :], 0.0))
        zeros_done = (s_const, s_const.count)

        mask_t = sb("mask_t", [P, P], BF16)
        const(lambda e: e.memset(mask_t[:, :], 0.0))
        const(lambda e: e.affine_select(out=mask_t[:, :], in_=mask_t[:, :], compare_op=ALU.is_ge, fill=NEG,
                                        base=0, pattern=[[1, P]], channel_multiplier=-1))
        mask_s = sb("mask_s", [P, P])
        const(lambda e: e.memset(mask_s[:, :], 0.0))
        const(lambda e: e.affine_select(out=mask_s[:, :], in_=mask_s[:, :], compare_op=ALU.is_ge, fill=NEG,
                                        base=0, pattern=[[-1, P]], channel_multiplier=1))
        before = sb("before", [P, P], BF16)
        const(lambda e: e.memset(before[:, :], 0.0))
        const(lambda e: e.affine_select(out=before[:, :], in_=before[:, :], compare_op=ALU.is_ge, fill=1.0,
                                        base=0, pattern=[[-1, P]], channel_multiplier=1))
        ones_bf = sb("ones_bf", [P, P], BF16)
        const(lambda e: e.memset(ones_bf[:, :], 1.0))
        zeros_bf = sb("zeros_bf", [P, QB], BF16)
        const(lambda e: e.memset(zeros_bf[:, :], 0.0))
        quads = sb("quads", [P, VW])
        const(lambda e: e.memset(quads[:, :], 0.0))
        for c in range(TPJ):
            const(lambda e, c=c: e.affine_select(out=quads[:, :], in_=quads[:, :], compare_op=ALU.not_equal,
                                                 fill=1.0, base=-32 * c, pattern=[[-1, VW]],
                                                 channel_multiplier=1))
        carry = sb("carry", [P, E, NT])
        const(lambda e: e.memset(carry[:, :, :], 1.0))
        const(lambda e: e.memset(carry[:, :, 0:1], 0.0))
        def iota(name, shape, pattern, mult=0, base=0):
            t = sb(name, shape)
            ti = sb(name + "_i", shape, I32)
            const(lambda e: e.iota(ti[:, :], pattern=pattern, base=base, channel_multiplier=mult))
            const(lambda e: e.tensor_copy(t[:, :], ti[:, :]))
            return t
        tile_steps = iota("tile_steps", [P, S // TILE], [[TILE, S // TILE]])
        tile_ids = iota("tile_ids", [P, N_TILES], [[1, N_TILES]])
        tile_col = iota("tile_col", [P, 1], [[0, 1]], mult=1)
        expert_ids = iota("expert_ids", [P, E], [[1, E]])
        expert_rank = iota("expert_rank", [P, E], [[-1, E]], base=E)
        ones_e = sb("ones_e", [P, E])
        const(lambda e: e.memset(ones_e[:, :], 1.0))
        consts_done = (s_const, s_const.count)

        GRP = 8
        x_loaded = []
        for g in range(NT // GRP):
            x_loaded.append(dma("sync", x_res[:, g * GRP:(g + 1) * GRP, :],
                                x_in.rearrange("(i p) d -> p i d", p=P)[:, g * GRP:(g + 1) * GRP, :],
                                [], sig(f"x_loaded{g}")))
        gate_w_sb = sb("gate_w_sb", [P, KD, E])
        gate_b_sb = sb("gate_b_sb", [P, E])
        s_small = sig("small_loads")
        dma("scalar", gate_w_sb[:, :, :], gate_w.rearrange("(k p) e -> p k e", p=P), [], s_small)
        small_loaded = dma("scalar", gate_b_sb[:, :], gate_b.partition_broadcast(P), [], s_small)
        s_attw = sig("attention_weights")
        dma("scalar", w_qkv_sb[:, :, :], w_qkv_t.rearrange("(k p) o -> p k o", p=P), [], s_attw)
        attw_loaded = dma("scalar", w_out_sb[:, :, :], w_out_t.rearrange("(k p) o -> p k o", p=P), [], s_attw)

        slots_zeroed = []
        per = N_TILES * TILE // P

        def zero_slots(f, waits):
            slots_zeroed.append(dma("scalar", slots[f].rearrange("(p r) d -> p r d", p=P),
                                    zero_row[:, :].unsqueeze(1).to_broadcast([P, per, ROW]),
                                    [zeros_done] + waits, sig(f"slots_zeroed{f}")))

        experts = phase[:, :].rearrange("p (e l w) -> p e l w", e=E, l=LAYERS)
        v_aug = phase[:, 0:NT * H * VW].rearrange("p (i h w) -> p i h w", i=NT, h=H)
        work = sb("work", [P, WORK])

        def load_experts(f, waits):
            s = sig(f"experts_loaded{f}")
            for l, w in enumerate((w1, w2, w3)):
                for k in range(KD):
                    m = dma("sync", experts[:, :, l, k * D:(k + 1) * D],
                            w.rearrange("e (k p) o -> p k e o", p=P)[:, k], waits, s)
            return dma("sync", experts[:, :, :, KD * D:WROW], bias_cols, waits, s)

        s_stat, s_eps, s_sqrt, s_rstd = sig("bn_stats"), sig("var_eps"), sig("sqrt"), sig("rstd")
        s_mv, s_norm, s_tr = sig("mean_var"), sig("normed"), sig("transposed")
        s_feat_a, s_feat_v = sig("feat_by_scalar"), sig("feat_by_vector")

        def layer_norm(x_ready, rows_free, feat_free):
            normed, feat_marks = [], []
            for g in range(NT // GRP):
                tiles = range(g * GRP, (g + 1) * GRP)
                for i in tiles:
                    st = put("vector", lambda e, i=i: e.bn_stats(stats[:, i, :], x_res[:, i, :]),
                             x_ready[i], s_stat)
                for i in tiles:
                    mv = put("vector", lambda e, i=i: e.bn_aggr(mean_var[:, i, :], stats[:, i, :]), [st], s_mv)
                a, b = g * GRP, (g + 1) * GRP
                ve = put("vector", lambda e, a=a, b=b: e.tensor_scalar(
                    rstd[:, 0, a:b], mean_var[:, a:b, 1], EPS, None, ALU.add), [mv], s_eps)
                sq = put("scalar", lambda e, a=a, b=b: e.activation(rstd[:, 1, a:b], rstd[:, 0, a:b], ACT.Sqrt),
                         [ve], s_sqrt)
                rs = put("vector", lambda e, a=a, b=b: e.reciprocal(rstd[:, 0, a:b], rstd[:, 1, a:b]), [sq], s_rstd)
                for i in tiles:
                    normed.append(put("vector", lambda e, i=i: e.tensor_scalar(
                        rows[:, i, 0:D], x_res[:, i, :], mean_var[:, i, 0:1], rstd[:, 0, i:i + 1],
                        ALU.subtract, ALU.mult), [rs, *rows_free], s_norm))
                for i0 in range(a, b, 4):
                    for k in range(KD):
                        n = (i0 // 4) * KD + k
                        bk = n % 4
                        for i in range(i0, i0 + 4):
                            tr = put("tensor", lambda e, i=i, k=k, bk=bk, i0=i0: e.transpose(
                                bank[bk][:, (i - i0) * P:(i - i0 + 1) * P], rows[:, i, k * P:(k + 1) * P],
                                ident[:, :]), [normed[i], consts_done, *free[bk]], s_tr)
                        if n % 2:
                            mk = put("vector", lambda e, k=k, bk=bk, i0=i0: e.tensor_copy(
                                feat[:, k, i0 * P:(i0 + 4) * P], bank[bk][:, :]), [tr, *feat_free], s_feat_v)
                        else:
                            mk = put("scalar", lambda e, k=k, bk=bk, i0=i0: e.activation(
                                feat[:, k, i0 * P:(i0 + 4) * P], bank[bk][:, :], ACT.Copy), [tr, *feat_free],
                                s_feat_a)
                        free[bk] = (mk,)
                        feat_marks.append(mk)
            return normed, feat_marks

        fat = [0]

        def fcarve(n):
            fat[0] += n
            return feat[:, 1, fat[0] - n:fat[0]]

        logits = fcarve(NT * E).rearrange("p (i e) -> p i e", e=E)
        probs = fcarve(NT * E).rearrange("p (i e) -> p i e", e=E)
        scratch = fcarve(4 * NT * E).rearrange("p (n i e) -> p n i e", n=4, e=E)
        sel = fcarve(TOP * NT * E).rearrange("p (n i e) -> p n i e", n=TOP, e=E)
        chosen = fcarve(NT * E).rearrange("p (i e) -> p i e", e=E)
        chosen_bf = sb("chosen_bf", [P, NT, E], BF16)
        small = sb("small", [P, 12, NT])
        per_expert = sb("per_expert", [P, 12, E])
        slot_no = sb("slot_no", [P, TOP, NT], U32)
        steps_gt = fcarve(E * S // TILE).rearrange("p (e t) -> p e t", e=E)
        tile_cmp = fcarve(N_TILES * E).rearrange("p (j e) -> p j e", e=E)
        tile_mask = fcarve(N_TILES * E).rearrange("p (j e) -> p j e", e=E)
        tile_exp = sb("tile_exp", [P, N_TILES])
        tile_exp_i = sb("tile_exp_i", [P, N_TILES], I32)
        tile_hot = sb("tile_hot", [P, 3, E])
        v_part = sb("v_part", [P, KD, N_TILES])
        v_rows = sb("v_rows", [P, D])
        v_half = sb("v_half", [P, D])
        s_gate, s_dve, s_gexp, s_ared = sig("gate_mm"), sig("routing"), sig("gate_exp"), sig("all_reduce")
        s_cnt, s_scat = sig("count_mm"), sig("scattered")
        s_cht, s_chc = sig("chosen_tr"), sig("chosen_copy")
        s_slot = [sig(f"slot_tile{i}") for i in range(3)]
        s_stage, s_xt, s_xtc, s_wb, s_wbt, s_wbc = (sig("staged"), sig("tile_tr"), sig("tile_copied"),
                                                     sig("weight_col"), sig("weight_tr"), sig("weight_row"))
        s_mm = [sig(f"layer_mm{l}") for l in range(LAYERS)]
        s_act_a, s_act_v = sig("relu_by_scalar"), sig("relu_by_vector")
        s_wy, s_vp = sig("weighted"), sig("v_partial")
        s_vt, s_vr, s_vm, s_vh, s_cmb, s_xadd = (sig("v_tr"), sig("v_rows"), sig("v_mm"), sig("v_half"),
                                                 sig("combine"), sig("x_added"))

        at = [0]

        def carve(n):
            at[0] += n
            assert at[0] <= WORK
            return work[:, at[0] - n:at[0]]

        NXG = 3
        W_RING = LAYERS + 1
        x_slot = carve(NXG * TS * ROW).rearrange("p (b u r) -> p b u r", b=NXG, u=TS)
        staged = carve(2 * LAYERS * WROW).rearrange("p (b l w) -> p b l w", b=2, l=LAYERS)
        acts = carve(3 * 2 * KD * TILE).rearrange("p (l b k s) -> p l b k s", l=3, b=2, k=KD)
        weighted = carve(2 * KD * TILE).rearrange("p (b m s) -> p b m s", b=2, m=KD)
        w_row = carve(W_RING * TILE).rearrange("p (b s) -> p b s", b=W_RING)
        w_wide = carve(2 * TS * P).rearrange("p (b u s) -> p b u s", b=2, u=TS)
        w_pick = carve(2 * TS * E).rearrange("p (b u e) -> p b u e", b=2, u=TS)
        w_col = carve(2 * TS).rearrange("p (b u) -> p b u", b=2)

        def bc(ap, axis, shape):
            return ap.unsqueeze(axis).to_broadcast(shape)

        def moe(f, x_ready, experts_loaded, work_free, rows_free, feat_free):
            normed, feat_marks = layer_norm(x_ready, rows_free, feat_free)
            PNE = [P, NT, E]

            gate_bank = bank[4]
            for i in range(NT):
                for k in range(KD):
                    g_mm = put("tensor", lambda e, i=i, k=k: e.matmul(
                        gate_bank[:, i * E:(i + 1) * E], feat[:, k, i * P:(i + 1) * P], gate_w_sb[:, k, :],
                        start=(k == 0), stop=(k == KD - 1)),
                        [small_loaded, *feat_marks[(i // 4) * KD:(i // 4) * KD + KD], *free[4]], s_gate)
            v_last = [None]

            def v(emit, *waits):
                v_last[0] = put("vector", emit, [v_last[0], *waits], s_dve)
                return v_last[0]

            gate_v = gate_bank[:, 0:NT * E].rearrange("p (i e) -> p i e", e=E)
            v(lambda e: e.tensor_tensor(logits[:, :, :], gate_v, bc(gate_b_sb[:, :], 1, PNE), ALU.add), g_mm)
            free[4] = (v_last[0],)
            pe = lambda n: per_expert[:, n, :]
            m = v(lambda e: e.tensor_reduce(pe(0), logits[:, :, :].rearrange("p i e -> p e i"), AX_X, ALU.max))
            m = put("gpsimd", lambda e: e.partition_all_reduce(pe(1), pe(0), P, REDUCE.max), [m], s_ared)
            m = v(lambda e: e.tensor_tensor(logits[:, :, :], logits[:, :, :], bc(pe(1), 1, PNE), ALU.subtract), m)
            m = put("scalar", lambda e: e.activation(probs[:, :, :], logits[:, :, :], ACT.Exp), [m], s_gexp)
            m = v(lambda e: e.tensor_reduce(pe(2), probs[:, :, :].rearrange("p i e -> p e i"), AX_X, ALU.add), m)
            m = put("gpsimd", lambda e: e.partition_all_reduce(pe(3), pe(2), P, REDUCE.add), [m], s_ared)
            v(lambda e: e.reciprocal(pe(4), pe(3)), m)
            v(lambda e: e.tensor_tensor(probs[:, :, :], probs[:, :, :], bc(pe(4), 1, PNE), ALU.mult))

            left = probs
            for c in range(TOP):
                top, rank = small[:, 2 * c, :], small[:, 2 * c + 1, :]
                v(lambda e, left=left, top=top: e.tensor_reduce(top, left[:, :, :], AX_X, ALU.max))
                v(lambda e, left=left, top=top: e.tensor_tensor(scratch[:, 0], left[:, :, :], bc(top, 2, PNE),
                                                                ALU.is_equal))
                v(lambda e: e.tensor_tensor(scratch[:, 1], scratch[:, 0], bc(expert_rank[:, :], 1, PNE), ALU.mult),
                  consts_done)
                v(lambda e, rank=rank: e.tensor_reduce(rank, scratch[:, 1], AX_X, ALU.max))
                v(lambda e, c=c, rank=rank: e.tensor_tensor(sel[:, c], scratch[:, 1], bc(rank, 2, PNE), ALU.is_equal))
                if c == 0:
                    v(lambda e: e.scalar_tensor_tensor(scratch[:, 2], sel[:, 0], -4.0, probs[:, :, :],
                                                       ALU.mult, ALU.add))
                    left = scratch[:, 2]
            v(lambda e: e.tensor_tensor(chosen[:, :, :], sel[:, 0], sel[:, 1], ALU.add))
            cb = v(lambda e: e.tensor_copy(chosen_bf[:, :, :], chosen[:, :, :]))
            w_done = v(lambda e: e.tensor_tensor(rows[:, :, D:ROW], chosen[:, :, :], probs[:, :, :], ALU.mult))

            flat = chosen_bf[:, :, :].rearrange("p i e -> p (i e)")
            put("tensor", lambda e: e.matmul(bank[5][:, 0:NT * E], before[:, :], flat, start=True, stop=True),
                [cb, *free[5]], s_cnt)
            cnt = put("tensor", lambda e: e.matmul(bank[6][:, 0:NT * E], ones_bf[:, :], flat, start=True,
                                                   stop=True), [*free[6]], s_cnt)
            for i0 in range(0, NT, 4):
                bk = (i0 // 4) % 2
                for i in range(i0, i0 + 4):
                    t = put("tensor", lambda e, i=i, i0=i0, bk=bk: e.transpose(
                        bank[bk][0:E, (i - i0) * P:(i - i0 + 1) * P], chosen[:, i, :], ident[:, :]),
                        [*free[bk]], s_cht)
                cp = put("scalar", lambda e, i0=i0, bk=bk: e.activation(
                    feat[0:E, 0, i0 * P:(i0 + 4) * P], bank[bk][0:E, :], ACT.Copy), [t, g_mm], s_chc)
                free[bk] = (cp,)
            chosen_t_done = cp

            em = scratch[:, 0].rearrange("p i e -> p (i e)").rearrange("p (e i) -> p e i", e=E)
            run = scratch[:, 1].rearrange("p i e -> p (i e)").rearrange("p (e i) -> p e i", e=E)
            prior = scratch[:, 2].rearrange("p i e -> p (i e)").rearrange("p (e i) -> p e i", e=E)
            v(lambda e: e.tensor_copy(em, bank[6][:, 0:NT * E].rearrange("p (i e) -> p e i", e=E)), cnt)
            free[6] = (v_last[0],)
            fl = lambda ap: ap.rearrange("p e i -> p (e i)")
            v(lambda e: e.tensor_tensor_scan(fl(run), fl(carry[:, :, :]), fl(em), 0.0, ALU.mult, ALU.add))
            v(lambda e: e.tensor_tensor(prior, run, em, ALU.subtract))
            SE = [P, E, S // TILE]
            v(lambda e: e.tensor_tensor(steps_gt[:, :, :], run[:, :, NT - 1:NT].to_broadcast(SE),
                                        bc(tile_steps[:, :], 1, SE), ALU.is_gt))
            v(lambda e: e.tensor_reduce(pe(5), steps_gt[:, :, :], AX_X, ALU.add))
            v(lambda e: e.tensor_tensor_scan(pe(6), ones_e[:, :], pe(5), 0.0, ALU.mult, ALU.add))
            v(lambda e: e.tensor_tensor(pe(7), pe(6), pe(5), ALU.subtract))
            v(lambda e: e.tensor_scalar(pe(8), pe(7), float(TILE), None, ALU.mult))
            v(lambda e: e.tensor_tensor(scratch[:, 3], bank[5][:, 0:NT * E].rearrange("p (i e) -> p i e", e=E),
                                        prior.rearrange("p e i -> p i e"), ALU.add))
            free[5] = (v_last[0],)
            v(lambda e: e.tensor_tensor(scratch[:, 3], scratch[:, 3], bc(pe(8), 1, PNE), ALU.add))
            slot_marks = []
            for c in range(TOP):
                v(lambda e, c=c: e.tensor_tensor(scratch[:, 0], sel[:, c], scratch[:, 3], ALU.mult))
                v(lambda e, c=c: e.tensor_reduce(small[:, 4 + c, :], scratch[:, 0], AX_X, ALU.add))
                slot_marks.append(v(lambda e, c=c: e.tensor_copy(slot_no[:, c, :], small[:, 4 + c, :])))
            TE = [P, N_TILES, E]
            v(lambda e: e.tensor_tensor(tile_cmp[:, :, :], bc(tile_ids[:, :], 2, TE), bc(pe(6), 1, TE), ALU.is_ge))
            v(lambda e: e.tensor_reduce(tile_exp[:, :], tile_cmp[:, :, :], AX_X, ALU.add))
            v(lambda e: e.tensor_scalar(tile_exp[:, :], tile_exp[:, :], float(E - 1), None, ALU.min))
            table = v(lambda e: e.tensor_copy(tile_exp_i[:, :], tile_exp[:, :]))
            masks = v(lambda e: e.tensor_tensor(tile_mask[:, :, :], bc(tile_exp[:, :], 2, TE),
                                                bc(expert_ids[:, :], 1, TE), ALU.is_equal))
            v(lambda e: e.tensor_scalar(tile_hot[:, 0, :], pe(7), tile_col[:, 0:1], None, ALU.is_le))
            v(lambda e: e.tensor_scalar(tile_hot[:, 1, :], pe(6), tile_col[:, 0:1], None, ALU.is_le))
            hot = v(lambda e: e.tensor_tensor(tile_hot[:, 2, :], tile_hot[:, 0, :], tile_hot[:, 1, :], ALU.subtract))

            for c in range(TOP):
                for i in range(NT):
                    scattered = put("gpsimd", lambda e, c=c, i=i: e.indirect_dma_start(
                        out=slots[f], out_offset=bass.IndirectOffsetOnAxis(ap=slot_no[:, c, i:i + 1], axis=0),
                        in_=rows[:, i, :], in_offset=None), [slot_marks[c], w_done, slots_zeroed[f]], s_scat, 16)

            xs = slots[f].rearrange("(j u p) r -> j p u r", u=TS, p=P)
            loaded, xt_done, xt_copied, w_ready = {}, {}, {}, {}
            stage_done = {(l, b): () for l in range(LAYERS) for b in range(2)}
            staged_marks, layer_marks, relu_marks = {}, {}, {}
            x_free = {}
            wy_marks, vp_marks, wide_read = {}, {}, {}
            expert_reg = {}

            def stage(j):
                for l in range(LAYERS):
                    def emit(e, j=j, l=l):
                        if l == 0:
                            expert_reg[j] = e.value_load(tile_exp_i[0:1, j:j + 1], min_val=0, max_val=E - 1)
                        return e.tensor_copy(staged[:, j % 2, l, :],
                                             experts[:, bass.ds(expert_reg[j], 1), l, :].rearrange("p a w -> p (a w)"))
                    staged_marks[j, l] = put("gpsimd", emit, [
                        table, experts_loaded, *work_free, layer_marks.get((j - 2, l)),
                        *relu_marks.get((j - 2, l), ())], s_stage)

            def load(j):
                loaded[j] = dma("sync", x_slot[:, j % NXG], xs[j], [scattered, *work_free, *x_free.get(j - NXG, ())],
                                s_slot[j % NXG])

            def transpose_tile(j):
                b = j % 2
                for u in range(TS):
                    for k in range(KD):
                        xt_done[j] = put("tensor", lambda e, j=j, u=u, k=k: e.transpose(
                            bank[0][:, k * TILE + u * P:k * TILE + (u + 1) * P],
                            x_slot[:, j % NXG, u, k * P:(k + 1) * P], ident[:, :]), [loaded[j], *free[0]], s_xt)
                pk = put("vector", lambda e, j=j, b=b: e.tensor_tensor(
                    w_pick[:, b], x_slot[:, j % NXG, :, D:ROW], bc(tile_mask[:, j, :], 1, [P, TS, E]), ALU.mult),
                    [loaded[j], masks, *work_free], s_wb)
                pk = put("vector", lambda e, b=b: e.tensor_reduce(w_col[:, b], w_pick[:, b], AX_X, ALU.add),
                         [pk], s_wb)
                wd = put("vector", lambda e, b=b: e.tensor_copy(w_wide[:, b], bc(w_col[:, b], 2, [P, TS, P])),
                         [pk, wide_read.get(j - 2)], s_wb)
                x_free[j] = (xt_done[j], pk)
                cp = put("scalar", lambda e, b=b: e.activation(
                    acts[:, 0, b].rearrange("p k s -> p (k s)"), bank[0][:, :], ACT.Copy),
                    [xt_done[j], layer_marks.get((j - 2, 0)), *work_free], s_xtc)
                free[0] = (cp,)
                xt_copied[j] = cp
                for u in range(TS):
                    wt = put("tensor", lambda e, u=u, b=b: e.transpose(
                        bank[1][:, u * P:(u + 1) * P], w_wide[:, b, u], ident[:, :]), [wd, *free[1]], s_wbt)
                w_ready[j] = put("scalar", lambda e, b=b: e.activation(w_row[:, j % W_RING], bank[1][:, 0:TILE],
                                                                      ACT.Copy),
                                 [wt, *wy_marks.get(j - W_RING, ()), *work_free], s_wbc)
                free[1] = (w_ready[j],)
                wide_read[j] = wt

            def layer(j, l):
                b = j % 2
                src = (xt_copied[j],) if l == 0 else relu_marks[j, l - 1]
                bk = 2 + l
                for m in range(KD):
                    for k in range(KD):
                        mm = put("tensor", lambda e, m=m, k=k: e.matmul(
                            bank[bk][:, m * TILE:(m + 1) * TILE],
                            staged[:, b, l, k * D + m * P:k * D + (m + 1) * P], acts[:, l, b, k],
                            start=(k == 0), stop=(k == KD - 1)),
                            [staged_marks[j, l], *src, *free[bk]], s_mm[l] if m == k == KD - 1 else None)
                layer_marks[j, l] = mm
                bias = lambda m: staged[:, b, l, KD * D + m:KD * D + m + 1]
                psum = lambda m: bank[bk][:, m * TILE:(m + 1) * TILE]
                if l < LAYERS - 1:
                    dst_free = layer_marks.get((j - 2, l + 1))
                    a = put("scalar", lambda e: e.activation(acts[:, l + 1, b, 0], psum(0), ACT.Relu, bias=bias(0)),
                            [mm, dst_free], s_act_a)
                    d = put("vector", lambda e: e.tensor_scalar(acts[:, l + 1, b, 1], psum(1), bias(1), 0.0,
                                                                ALU.add, ALU.max), [a, dst_free], s_act_v)
                    relu_marks[j, l] = (a, d)
                    free[bk] = (a, d)
                else:
                    for m in range(KD):
                        wy = put("vector", lambda e, m=m: e.scalar_tensor_tensor(
                            weighted[:, b, m], psum(m), bias(m), w_row[:, j % W_RING], ALU.add, ALU.mult),
                            [mm, w_ready[j], *vp_marks.get(j - 2, ())], s_wy)
                        vp = put("scalar", lambda e, m=m: e.activation(
                            weighted[:, b, m], weighted[:, b, m], ACT.Relu, accum_out=v_part[:, m, j:j + 1]),
                            [wy], s_vp)
                    free[bk] = (wy,)
                    relu_marks[j, l] = (wy,)
                    wy_marks[j] = (wy,)
                    vp_marks[j] = (vp,)

            stage(0)
            load(0)
            load(1)
            for j in range(N_TILES + 3):
                if j + 1 < N_TILES:
                    stage(j + 1) if j + 1 < 2 else None
                if j + 2 < N_TILES:
                    load(j + 2)
                if j < N_TILES:
                    transpose_tile(j)
                if 0 <= j - 3 < N_TILES:
                    layer(j - 3, 2)
                    if j - 3 + 2 < N_TILES:
                        stage(j - 3 + 2)
                if 0 <= j - 2 < N_TILES:
                    layer(j - 2, 1)
                if 0 <= j - 1 < N_TILES:
                    layer(j - 1, 0)
            work_done = [layer_marks[N_TILES - 1, 2], *wy_marks[N_TILES - 1], *vp_marks[N_TILES - 1],
                         staged_marks[N_TILES - 1, LAYERS - 1]]

            for m in range(KD):
                t = put("tensor", lambda e, m=m: e.transpose(bank[5][0:N_TILES, m * P:(m + 1) * P],
                                                             v_part[:, m, :], ident[:, :]),
                        [*vp_marks[N_TILES - 1], *free[5]], s_vt)
            c = put("vector", lambda e: e.tensor_copy(v_rows[0:N_TILES, :], bank[5][0:N_TILES, 0:D]), [t], s_vr)
            free[5] = (c,)
            t = put("tensor", lambda e: e.matmul(bank[6][0:E, 0:D], tile_hot[0:N_TILES, 2, :], v_rows[0:N_TILES, :],
                                                 start=True, stop=True), [c, hot, *free[6]], s_vm)
            vh = put("vector", lambda e: e.tensor_scalar(v_half[0:E, :], bank[6][0:E, 0:D], 0.5, None, ALU.mult),
                     [t], s_vh)
            free[6] = (vh,)
            x_marks = []
            for i0 in range(0, NT, 2):
                bk = (i0 // 2) % 3 if True else 0
                for i in (i0, i0 + 1):
                    cm = put("tensor", lambda e, i=i, i0=i0, bk=bk: e.matmul(
                        bank[bk][:, (i - i0) * D:(i - i0 + 1) * D], feat[0:E, 0, i * P:(i + 1) * P], v_half[0:E, :],
                        start=True, stop=True), [vh, chosen_t_done, *free[bk]], s_cmb)
                xm = put("vector", lambda e, i0=i0, bk=bk: e.tensor_tensor(
                    x_res[:, i0:i0 + 2, :], x_res[:, i0:i0 + 2, :],
                    bank[bk][:, :].rearrange("p (a d) -> p a d", a=2), ALU.add), [cm], s_xadd)
                free[bk] = (xm,)
                x_marks += [xm, xm]
            return dict(x=x_marks, work=work_done, rows=[scattered], feat=[cm], phase=[staged_marks[N_TILES - 1, 2]])

        def attention(x_ready, work_free, phase_free, rows_free, feat_free):
            at[0] = 0
            bf = lambda ap: ap.bitcast(BF16)
            stack = bf(carve(2 * 2 * S // 2)).rearrange("p (b c s) -> p b c s", b=2, c=2)
            maxima = carve(2 * NJ * TPJ * (NJ + 1)).rearrange("p (b j i c) -> p b j i c", b=2, j=NJ, i=TPJ)
            neg_max = carve(4 * TPJ).rearrange("p (b i) -> p b i", b=4)
            max_parts = bf(carve(4 * TPJ * M_PARTS // 2)).rearrange("p (b i m) -> p b i m", b=4, i=TPJ)
            recip = carve(2 * TPJ).rearrange("p (b i) -> p b i", b=2)
            p_ring = feat[:, 0, :].rearrange("p (r s) -> p r s", r=P_RING)
            acc_sb = feat[:, 1, 0:2 * QB].rearrange("p (b s) -> p b s", b=2)
            v_end = NT * H * VW
            split_bf = bf(phase[:, v_end:v_end + 2 * 3 * QB // 2]).rearrange("p (b t s) -> p b t s", b=2, t=3)
            split_f = phase[:, v_end + 3 * QB:v_end + 5 * QB].rearrange("p (b s) -> p b s", b=2)
            heads = rows[:, :, 0:D]

            normed, feat_marks = layer_norm(x_ready, rows_free, feat_free)

            s_pm, s_p1, s_r1, s_p2, s_p3 = (sig("proj_mm"), sig("part1"), sig("rest1"), sig("part2"), sig("part3"))
            s_wr = [sig(f"parts_stored{i}") for i in range(2)]
            parts_stored = {}
            store = {}
            p3m, r1m = {}, {}

            def project_chunk(ob, sc):
                n = len(store)
                bk, b = n % 4, n % 2
                for k in range(KD):
                    mm = put("tensor", lambda e, k=k: e.matmul(
                        bank[bk][:, :], w_qkv_sb[:, k, ob * P:(ob + 1) * P], feat[:, k, sc * QB:(sc + 1) * QB],
                        start=(k == 0), stop=(k == KD - 1)),
                        [attw_loaded, *feat_marks[sc * KD:(sc + 1) * KD], *free[bk]], s_pm)
                p1 = put("scalar", lambda e: e.activation(split_bf[:, b, 0], bank[bk][:, :], ACT.Copy),
                         [mm, store.get(n - 2), *phase_free], s_p1)
                r1 = put("vector", lambda e: e.tensor_tensor(split_f[:, b], bank[bk][:, :], split_bf[:, b, 0],
                                                             ALU.subtract),
                         [p1, p3m.get(n - 2), *phase_free], s_r1)
                free[bk] = (r1,)
                p2 = put("scalar", lambda e: e.activation(split_bf[:, b, 1], split_f[:, b], ACT.Copy), [r1], s_p2)
                p3m[n] = put("gpsimd", lambda e: e.tensor_tensor(split_bf[:, b, 2], split_f[:, b],
                                                                 split_bf[:, b, 1], ALU.subtract),
                             [p2, store.get(n - 2)], s_p3)
                qk, r0 = ob // KD, (ob % KD) * P
                store[n] = dma("sync", parts_dram[qk, :, r0:r0 + P, sc * QB:(sc + 1) * QB]
                               .rearrange("t r s -> r t s"), split_bf[:, b], [p3m[n], p1, p2], s_wr[b])

            def project(ob):
                for sc in range(NJ):
                    project_chunk(ob, sc)
                n = len(store)
                parts_stored[ob] = (store[n - 2], store[n - 1])

            s_stack = [sig(f"stack{i}") for i in range(2)]
            stack_loaded = {}
            b_last = {}

            def load_stack(h):
                half = h // (H // KD)
                waits = [*parts_stored[half], *parts_stored[KD + half], *work_free,
                         b_last.get(h - 2)]
                for r, pair in enumerate(PARTS):
                    for c in range(2):
                        stack_loaded[h] = dma("sync", stack[r * HD:(r + 1) * HD, h % 2, c, :],
                                              parts_dram[c, pair[c], h * HD:(h + 1) * HD, :], waits, s_stack[h % 2])

            project(0)
            project(KD)
            load_stack(0)
            load_stack(1)

            s_vmm, s_vcp, s_ones = sig("v_mm_"), sig("v_copied"), sig("ones_set")
            put("vector", lambda e: e.memset(v_aug[:, :, :, HD:VW], 1.0), [*phase_free], s_ones)
            for b in range(2):
                ones_set = put("vector", lambda e, b=b: e.memset(
                    stack[QK_ROWS:QK_ROWS + M_PARTS, b, 1, :], 1.0), [*work_free], s_ones)
            for i in range(NT):
                bk = 4 + i % 2
                for k in range(KD):
                    mm = put("tensor", lambda e, k=k, i=i, bk=bk: e.matmul(
                        bank[bk][:, 0:D], feat[:, k, i * P:(i + 1) * P], w_qkv_sb[:, k, 2 * D:3 * D],
                        start=(k == 0), stop=(k == KD - 1)), [*free[bk]], s_vmm)
                v_copied = put("scalar", lambda e, i=i, bk=bk: e.activation(
                    v_aug[:, i, :, 0:HD], bank[bk][:, 0:D].rearrange("p (h d) -> p h d", h=H), ACT.Copy),
                    [mm, *phase_free], s_vcp)
                free[bk] = (v_copied,)
            project(1)
            project(KD + 1)
            feat_read = (s_pm, s_pm.count)

            s_s, s_e, s_pv, s_acc, s_sum, s_rl, s_head = (sig("scores_t"), sig("exp"), sig("pv"), sig("acc_copied"),
                                                          sig("quads_summed"), sig("recip"), sig("head_out"))
            s_a, s_mx, s_neg, s_mp, s_mt, s_mrow = (sig("scores"), sig("max_part"), sig("neg_max"),
                                                    sig("max_parts"), sig("max_tr"), sig("max_row"))
            put("tensor", lambda e: e.matmul(bank[ACC_BANK][:, :], zeros_bf[:, 0:P], zeros_bf[:, :], start=True,
                                             stop=True), [*free[ACC_BANK]], s_pv)
            mx_set = put("vector", lambda e: e.memset(maxima, NEG), [*work_free], s_ones)

            units = [(h, j) for h in range(H) for j in range(NJ)]
            a_items = [(h, j, i, c) for h, j in units for i in range(TPJ) for c in range(j + 1)]
            b_items = [(h, j, t) for h, j in units for t in range(TPJ * (j + 1))]
            assert len(a_items) == len(b_items)
            mrow_done, neg_done, p_marks, exp_marks, pv_marks, mp_marks = {}, {}, {}, {}, {}, {}

            def a_item(n):
                h, j, i, c = a_items[n]
                bk = A_BANKS[n % len(A_BANKS)]
                w = QB if c < j else (i + 1) * P
                q0 = (TPJ * j + i) * P
                mm = put("tensor", lambda e: e.matmul(
                    bank[bk][:, 0:w], stack[0:QK_ROWS, h % 2, 0, q0:q0 + P], stack[0:QK_ROWS, h % 2, 1, c * QB:c * QB + w],
                    start=True, stop=True), [stack_loaded[h], *free[bk]], s_a)
                col = lambda k: maxima[:, h % 2, j, i, k:k + 1]
                last = None
                prev = neg_done.get((h - 2, j))
                full = w if c < j else w - P
                if full:
                    last = put("vector", lambda e: e.tensor_reduce(col(c if c < j else NJ), bank[bk][:, 0:full], AX_X, ALU.max),
                               [mm, mx_set, prev], s_mx)
                if c == j:
                    last = put("vector", lambda e: e.tensor_tensor_reduce(
                        bank[bk][:, w - P:w], bank[bk][:, w - P:w], mask_s[:, :], 1.0, NEG, ALU.add, ALU.max,
                        col(c)), [mm, mx_set, prev, consts_done], s_mx)
                free[bk] = (last,)
                if i == TPJ - 1 and c == j:
                    u = h * NJ + j
                    neg_done[h, j] = put("vector", lambda e: e.tensor_reduce(
                        neg_max[:, u % 4, :], maxima[:, h % 2, j], AX_X, ALU.max, negate=True),
                        [last, mp_marks.get(u - 4)], s_neg)
                    m1 = put("gpsimd", lambda e: e.tensor_copy(max_parts[:, u % 4, :, 0], neg_max[:, u % 4, :]),
                             [neg_done[h, j], mt_marks.get(u - 4)], s_mp)
                    mp_marks[u] = put("gpsimd", lambda e: e.tensor_tensor(
                        max_parts[:, u % 4, :, 1], neg_max[:, u % 4, :], max_parts[:, u % 4, :, 0], ALU.subtract),
                        [m1], s_mp)
                    return u
                return None

            mt_marks = {}

            def max_row(u):
                h, j = units[u]
                for i in range(TPJ):
                    mt_marks[u] = put("tensor", lambda e, i=i: e.matmul(
                        bank[M_BANK][QK_ROWS:QK_ROWS + M_PARTS, i * P:(i + 1) * P], max_parts[:, u % 4, i, :],
                        ident_bf[:, :], start=True, stop=True), [mp_marks[u], *free[M_BANK]], s_mt)
                mrow_done[u] = put("scalar", lambda e: e.activation(
                    stack[QK_ROWS:QK_ROWS + M_PARTS, h % 2, 0, j * QB:(j + 1) * QB],
                    bank[M_BANK][QK_ROWS:QK_ROWS + M_PARTS, :], ACT.Copy), [mt_marks[u], b_last.get(h - 2)], s_mrow)
                free[M_BANK] = (mrow_done[u],)

            def b_item(n):
                h, j, t = b_items[n]
                u = h * NJ + j
                bk = S_BANKS[n % len(S_BANKS)]
                diag = t - TPJ * j
                lo = max(diag, 0) * P
                mm = put("tensor", lambda e: e.matmul(
                    bank[bk][:, lo:QB], stack[0:QK_ROWS + M_PARTS, h % 2, 1, t * P:(t + 1) * P],
                    stack[0:QK_ROWS + M_PARTS, h % 2, 0, j * QB + lo:(j + 1) * QB], start=True, stop=(diag < 0)),
                    [mrow_done[u], stack_loaded[h], ones_set, *free[bk]], s_s)
                if diag >= 0:
                    mm = put("tensor", lambda e: e.matmul(bank[bk][:, lo:lo + P], ident_bf[:, :], mask_t[:, :],
                                                          start=False, stop=True), [], s_s)
                b_last[h] = mm
                exp_marks[n] = put("scalar", lambda e: e.activation(
                    p_ring[:, n % P_RING, lo:QB], bank[bk][:, lo:QB], ACT.Exp, scale=HD ** -0.5),
                    [mm, pv_marks.get(n - P_RING), feat_read], s_e)
                free[bk] = (exp_marks[n],)

            def pv_group(n0):
                h, j, t0 = b_items[n0]
                u = h * NJ + j
                first = t0 == 0
                zero_start = first and j == 0
                if zero_start:
                    for c in range(TPJ):
                        put("tensor", lambda e, c=c: e.matmul(
                            bank[ACC_BANK][32 * c:32 * c + VW, :], zeros_bf[:, 0:VW], zeros_bf[:, :],
                            start=True, stop=False), [*free[ACC_BANK]], s_pv)
                for c in range(TPJ):
                    t = t0 + c
                    lo = max(t - TPJ * j, 0) * P
                    pv_marks[n0 + c] = put("tensor", lambda e, c=c, t=t, lo=lo: e.matmul(
                        bank[ACC_BANK][32 * c:32 * c + VW, lo:QB], v_aug[:, t, h, :], p_ring[:, (n0 + c) % P_RING, lo:QB],
                        start=(first and not zero_start), stop=(t0 == TPJ * j)),
                        [exp_marks[n0 + c], v_copied, ones_set, *free[ACC_BANK]], s_pv)
                if t0 == TPJ * j:
                    cp = put("scalar", lambda e: e.activation(acc_sb[:, u % 2, :], bank[ACC_BANK][:, :], ACT.Copy),
                             [pv_marks[n0 + TPJ - 1], sum_marks.get(u - 2), feat_read], s_acc)
                    free[ACC_BANK] = (cp,)
                    return u, cp
                return None

            sum_marks = {}
            head_marks = []

            def finish_unit(u, cp):
                h, j = units[u]
                for i in range(TPJ):
                    sum_marks[u] = put("tensor", lambda e, i=i: e.matmul(
                        bank[O_BANK][:, i * 32:i * 32 + VW], acc_sb[:, u % 2, i * P:(i + 1) * P], quads[:, :],
                        start=True, stop=True), [cp, *free[O_BANK]], s_sum)
                o = bank[O_BANK][:, 0:TPJ * 32].rearrange("p (i w) -> p i w", w=32)
                rl = put("vector", lambda e: e.reciprocal(recip[:, u % 2, :], o[:, :, HD]),
                         [sum_marks[u], head_marks[-2] if u >= 2 else None], s_rl)
                hm = put("vector", lambda e: e.tensor_tensor(
                    heads[:, TPJ * j:TPJ * (j + 1), h * HD:(h + 1) * HD], o[:, :, 0:HD],
                    bc(recip[:, u % 2, :], 2, [P, TPJ, HD]), ALU.mult), [rl], s_head)
                free[O_BANK] = (hm,)
                head_marks.append(hm)

            due = {}
            total = len(a_items)
            pending_pv, pending_fin = [], []
            for n in range(total + LEAD):
                if n < total:
                    u = a_item(n)
                    if u is not None:
                        due.setdefault(n + 5, []).append(u)
                for u in due.pop(n, []):
                    max_row(u)
                bn = n - LEAD
                if bn >= 0:
                    h, j, t = b_items[bn]
                    if j == 2 and t == 0 and 1 <= h < H - 1:
                        load_stack(h + 1)
                    b_item(bn)
                    if bn % TPJ == TPJ - 1:
                        if pending_fin:
                            finish_unit(*pending_fin.pop(0))
                        if pending_pv:
                            fin = pv_group(pending_pv.pop(0))
                            if fin:
                                pending_fin.append(fin)
                        pending_pv.append(bn - TPJ + 1)
            while pending_fin:
                finish_unit(*pending_fin.pop(0))
            finish_unit(*pv_group(pending_pv.pop(0)))
            all_heads = head_marks[-1]
            last_pv = pv_marks[total - 1]

            s_ht, s_hc, s_hcv, s_om, s_xo = (sig("heads_tr"), sig("heads_copied"), sig("heads_copied_v"),
                                             sig("out_mm"), sig("x_attended"))
            x_marks = []
            for i0 in range(0, NT, 4):
                cps = []
                for k in range(KD):
                    bk = ((i0 // 4) * KD + k) % 4
                    for i in range(i0, i0 + 4):
                        tr = put("tensor", lambda e, i=i, k=k, bk=bk, i0=i0: e.transpose(
                            bank[bk][:, (i - i0) * P:(i - i0 + 1) * P], rows[:, i, k * P:(k + 1) * P], ident[:, :]),
                            [all_heads, *free[bk]], s_ht)
                    if k:
                        cp = put("vector", lambda e, k=k, bk=bk, i0=i0: e.tensor_copy(
                            feat[:, k, i0 * P:(i0 + 4) * P], bank[bk][:, :]), [tr, last_pv, sum_marks[len(units) - 1]], s_hcv)
                    else:
                        cp = put("scalar", lambda e, k=k, bk=bk, i0=i0: e.activation(
                            feat[:, k, i0 * P:(i0 + 4) * P], bank[bk][:, :], ACT.Copy), [tr, last_pv, sum_marks[len(units) - 1]], s_hc)
                    free[bk] = (cp,)
                    cps.append(cp)
                for i2 in range(i0, i0 + 4, 2):
                    bk = 4 + (i2 // 2) % 4
                    for i in (i2, i2 + 1):
                        for k in range(KD):
                            mm = put("tensor", lambda e, i=i, i2=i2, k=k, bk=bk: e.matmul(
                                bank[bk][:, (i - i2) * D:(i - i2 + 1) * D], feat[:, k, i * P:(i + 1) * P],
                                w_out_sb[:, k, :], start=(k == 0), stop=(k == KD - 1)), [*cps, *free[bk]], s_om)
                    xm = put("vector", lambda e, i2=i2, bk=bk: e.tensor_tensor(
                        x_res[:, i2:i2 + 2, :], x_res[:, i2:i2 + 2, :],
                        bank[bk][:, :].rearrange("p (a d) -> p a d", a=2), ALU.add), [mm], s_xo)
                    free[bk] = (xm,)
                    x_marks += [xm, xm]
            return dict(x=x_marks, work=[last_pv], phase=[last_pv], rows=[tr], feat=[mm])


        experts0 = load_experts(0, [])
        zero_slots(0, [])
        x_ready = [[x_loaded[i // GRP]] for i in range(NT)]
        if True:
            r = moe(0, x_ready, experts0, [], [], [])
            zero_slots(1, [r["work"][0]])
            r = attention([[m] for m in r["x"]], r["work"], r["phase"], r["rows"], r["feat"])
            experts1 = load_experts(1, r["phase"])
            r = moe(1, [[m] for m in r["x"]], experts1, r["work"], r["rows"], r["feat"])
        s_out = sig("stored")
        out_t = out.rearrange("(i p) d -> p i d", p=P)
        for g in range(NT // GRP):
            stored = dma("sync", out_t[:, g * GRP:(g + 1) * GRP, :], x_res[:, g * GRP:(g + 1) * GRP, :],
                         [r["x"][(g + 1) * GRP - 1]], s_out)
        q.lists["sync"].append(((stored,), lambda e: e.nop(), None, 0))

        block = ctx.enter_context(nc.Block())

        @block.sync
        def _(eng):
            q.run("sync", eng)

        @block.gpsimd
        def _(eng):
            q.run("gpsimd", eng)

        @block.scalar
        def _(eng):
            q.run("scalar", eng)

        @block.tensor
        def _(eng):
            q.run("tensor", eng)

        @block.vector
        def _(eng):
            q.run("vector", eng)


def kernel(**inputs):
    import numpy as np
    import concourse.bacc as bacc
    from concourse.bass_utils import run_bass_kernel_spmd

    given = {name: np.asarray(a) for name, a in inputs.items()}
    arrays = {
        "x": given["L0_attn_x"].reshape(S, D),
        "w_qkv_t": given["L0_attn_w_qkv"].T,
        "w_out_t": given["L0_attn_w_out"].T,
    }
    for name in ("gate_w", "gate_b", "w1", "w2", "w3"):
        arrays[name] = given["L0_ffn_" + name]
    biases = np.stack([given["L0_ffn_" + name] for name in ("b1", "b2", "b3")], axis=1)
    arrays["bias_cols"] = biases.reshape(E, LAYERS, KD, P).transpose(3, 0, 1, 2)
    arrays = {name: np.ascontiguousarray(a) for name, a in arrays.items()}
    nc = bacc.Bacc("TRN2", target_bir_lowering=False, num_devices=1)
    args = [nc.dram_tensor("in_" + name, a.shape, F32, kind="ExternalInput").ap() for name, a in arrays.items()]
    out = nc.dram_tensor("out", (S, D), F32, kind="ExternalOutput").ap()
    macaron_block(nc, *args, out)
    r = run_bass_kernel_spmd(nc, [{"in_" + name: a for name, a in arrays.items()}], core_ids=[0])
    return r.results[0]["out"].reshape(1, S, D)
```

```python
from contextlib import ExitStack

import concourse.bass as bass
from concourse import mybir

F32 = mybir.dt.float32
BF16 = mybir.dt.bfloat16
U32 = mybir.dt.uint32
I32 = mybir.dt.int32
ALU = mybir.AluOpType
ACT = mybir.ActivationFunctionType
AX_X = mybir.AxisListType.X
REDUCE = bass.bass_isa.ReduceOp

P = 128
S = 4096
D = 256
NT = S // P
KD = D // P
H = 16
HD = D // H
E = 8
LAYERS = 3
TOP = 2
EPS = 1e-5
NEG = -3.0e38

TILE = 256
TS = TILE // P
N_TILES = (TOP * S + E * (TILE - 1)) // TILE
ROW = D + E
WROW = KD * D + KD

QB = 512
NJ = S // QB
TPJ = QB // P
PARTS = ((0, 0), (0, 1), (0, 2), (1, 0), (1, 1), (2, 0))
QK_ROWS = len(PARTS) * HD
M_PARTS = 2
VW = HD + 1
S_BANKS = (0, 1, 2)
A_BANKS = (3, 4, 7)
ACC_BANK, M_BANK, O_BANK = 5, 6, 6
WORK = 10368
P_RING = 8
SPLIT = 4
LEAD = 44


class Counter:

    def __init__(self, sem):
        self.sem, self.count = sem, 0


class Queues:

    def __init__(self, nc, ctx):
        self.nc, self.ctx = nc, ctx
        self.lists = {name: [] for name in ("tensor", "vector", "scalar", "gpsimd", "sync")}

    def counter(self, name):
        return Counter(self.ctx.enter_context(self.nc.semaphore(name)))

    def put(self, engine, emit, waits=(), counter=None, amount=1):
        mark = None
        if counter is not None:
            counter.count += amount
            mark = (counter, counter.count)
        self.lists[engine].append((tuple(w for w in waits if w is not None), emit, counter, amount))
        return mark

    def dma(self, engine, out, in_, waits, counter):
        return self.put(engine, lambda e: e.dma_start(out, in_), waits, counter, 16)

    def run(self, engine, eng):
        reached = {}
        for waits, emit, counter, amount in self.lists[engine]:
            for s, value in waits:
                if reached.get(s, 0) < value:
                    eng.wait_ge(s.sem, value)
                    reached[s] = value
            ins = emit(eng)
            if counter is not None:
                ins.then_inc(counter.sem, amount)


def macaron_block(nc, x_in, w_qkv_t, w_out_t, gate_w, gate_b, w1, w2, w3, bias_cols, out):
    with ExitStack() as ctx:
        q = Queues(nc, ctx)
        sig, put, dma = q.counter, q.put, q.dma

        def sb(name, shape, dt=F32):
            return ctx.enter_context(nc.sbuf_tensor(name, shape, dt))

        x_res = sb("x_res", [P, NT, D])
        rows = sb("rows", [P, NT, ROW])
        feat = sb("feat", [P, KD, S])
        phase = sb("phase", [P, E * LAYERS * WROW])
        ident = sb("ident", [P, P])
        ident_bf = sb("ident_bf", [P, P], BF16)
        stats = sb("stats", [P, NT, 6])
        mean_var = sb("mean_var", [P, NT, 2])
        rstd = sb("rstd", [P, 2, NT])
        w_qkv_sb = sb("w_qkv_sb", [P, KD, 3 * D])
        w_out_sb = sb("w_out_sb", [P, KD, D])
        zero_row = sb("zero_row", [P, ROW])
        bank = [ctx.enter_context(nc.psum_tensor(f"bank{i}", [P, 512], F32)) for i in range(8)]
        free = {i: () for i in range(8)}

        slots = [nc.dram_tensor(f"slots{f}", (N_TILES * TILE, ROW), F32).ap() for f in range(2)]
        parts_dram = nc.dram_tensor("qk_parts", (2, 3, D, S), BF16).ap()

        s_const = sig("constants")

        def const(emit):
            last = (s_const, s_const.count) if s_const.count else None
            return put("gpsimd", emit, [last], s_const)

        def diagonal(t, n=P):
            const(lambda e: e.memset(t, 0.0))
            const(lambda e: e.affine_select(out=t, in_=t, compare_op=ALU.not_equal, fill=1.0, base=0,
                                            pattern=[[-1, n]], channel_multiplier=1))

        diagonal(ident[:, :])
        diagonal(ident_bf[:, :])
        const(lambda e: e.memset(zero_row[:, :], 0.0))
        zeros_done = (s_const, s_const.count)

        mask_t = sb("mask_t", [P, P], BF16)
        const(lambda e: e.memset(mask_t[:, :], 0.0))
        const(lambda e: e.affine_select(out=mask_t[:, :], in_=mask_t[:, :], compare_op=ALU.is_ge, fill=NEG,
                                        base=0, pattern=[[1, P]], channel_multiplier=-1))
        mask_s = sb("mask_s", [P, P])
        const(lambda e: e.memset(mask_s[:, :], 0.0))
        const(lambda e: e.affine_select(out=mask_s[:, :], in_=mask_s[:, :], compare_op=ALU.is_ge, fill=NEG,
                                        base=0, pattern=[[-1, P]], channel_multiplier=1))
        before = sb("before", [P, P], BF16)
        const(lambda e: e.memset(before[:, :], 0.0))
        const(lambda e: e.affine_select(out=before[:, :], in_=before[:, :], compare_op=ALU.is_ge, fill=1.0,
                                        base=0, pattern=[[-1, P]], channel_multiplier=1))
        ones_bf = sb("ones_bf", [P, P], BF16)
        const(lambda e: e.memset(ones_bf[:, :], 1.0))
        zeros_bf = sb("zeros_bf", [P, QB], BF16)
        const(lambda e: e.memset(zeros_bf[:, :], 0.0))
        carry = sb("carry", [P, E, NT])
        const(lambda e: e.memset(carry[:, :, :], 1.0))
        const(lambda e: e.memset(carry[:, :, 0:1], 0.0))
        def iota(name, shape, pattern, mult=0, base=0):
            t = sb(name, shape)
            ti = sb(name + "_i", shape, I32)
            const(lambda e: e.iota(ti[:, :], pattern=pattern, base=base, channel_multiplier=mult))
            const(lambda e: e.tensor_copy(t[:, :], ti[:, :]))
            return t
        tile_steps = iota("tile_steps", [P, S // TILE], [[TILE, S // TILE]])
        tile_ids = iota("tile_ids", [P, N_TILES], [[1, N_TILES]])
        tile_col = iota("tile_col", [P, 1], [[0, 1]], mult=1)
        expert_ids = iota("expert_ids", [P, E], [[1, E]])
        expert_rank = iota("expert_rank", [P, E], [[-1, E]], base=E)
        ones_e = sb("ones_e", [P, E])
        const(lambda e: e.memset(ones_e[:, :], 1.0))
        consts_done = (s_const, s_const.count)

        GRP = 8
        x_loaded = []
        for g in range(NT // GRP):
            x_loaded.append(dma("sync", x_res[:, g * GRP:(g + 1) * GRP, :],
                                x_in.rearrange("(i p) d -> p i d", p=P)[:, g * GRP:(g + 1) * GRP, :],
                                [], sig(f"x_loaded{g}")))
        gate_w_sb = sb("gate_w_sb", [P, KD, E])
        gate_b_sb = sb("gate_b_sb", [P, E])
        s_small = sig("small_loads")
        dma("scalar", gate_w_sb[:, :, :], gate_w.rearrange("(k p) e -> p k e", p=P), [], s_small)
        small_loaded = dma("scalar", gate_b_sb[:, :], gate_b.partition_broadcast(P), [], s_small)
        s_attw = sig("attention_weights")
        dma("scalar", w_qkv_sb[:, :, :], w_qkv_t.rearrange("(k p) o -> p k o", p=P), [], s_attw)
        attw_loaded = dma("scalar", w_out_sb[:, :, :], w_out_t.rearrange("(k p) o -> p k o", p=P), [], s_attw)

        slots_zeroed = []
        per = N_TILES * TILE // P

        def zero_slots(f, waits):
            slots_zeroed.append(dma("scalar", slots[f].rearrange("(p r) d -> p r d", p=P),
                                    zero_row[:, :].unsqueeze(1).to_broadcast([P, per, ROW]),
                                    [zeros_done] + waits, sig(f"slots_zeroed{f}")))

        experts = phase[:, :].rearrange("p (e l w) -> p e l w", e=E, l=LAYERS)
        v_aug = phase[:, 0:NT * H * VW].rearrange("p (i h w) -> p i h w", i=NT, h=H)
        work = sb("work", [P, WORK])

        def load_experts(f, waits):
            s = sig(f"experts_loaded{f}")
            for l, w in enumerate((w1, w2, w3)):
                for k in range(KD):
                    m = dma("sync", experts[:, :, l, k * D:(k + 1) * D],
                            w.rearrange("e (k p) o -> p k e o", p=P)[:, k], waits, s)
            return dma("sync", experts[:, :, :, KD * D:WROW], bias_cols, waits, s)

        s_stat, s_eps, s_sqrt, s_rstd = sig("bn_stats"), sig("var_eps"), sig("sqrt"), sig("rstd")
        s_mv, s_norm, s_tr = sig("mean_var"), sig("normed"), sig("transposed")
        s_feat_a, s_feat_v = sig("feat_by_scalar"), sig("feat_by_vector")

        def layer_norm(x_ready, rows_free, feat_free):
            normed, feat_marks = [], []
            for g in range(NT // GRP):
                tiles = range(g * GRP, (g + 1) * GRP)
                for i in tiles:
                    st = put("vector", lambda e, i=i: e.bn_stats(stats[:, i, :], x_res[:, i, :]),
                             x_ready[i], s_stat)
                for i in tiles:
                    mv = put("vector", lambda e, i=i: e.bn_aggr(mean_var[:, i, :], stats[:, i, :]), [st], s_mv)
                a, b = g * GRP, (g + 1) * GRP
                ve = put("vector", lambda e, a=a, b=b: e.tensor_scalar(
                    rstd[:, 0, a:b], mean_var[:, a:b, 1], EPS, None, ALU.add), [mv], s_eps)
                sq = put("scalar", lambda e, a=a, b=b: e.activation(rstd[:, 1, a:b], rstd[:, 0, a:b], ACT.Sqrt),
                         [ve], s_sqrt)
                rs = put("vector", lambda e, a=a, b=b: e.reciprocal(rstd[:, 0, a:b], rstd[:, 1, a:b]), [sq], s_rstd)
                for i in tiles:
                    normed.append(put("vector", lambda e, i=i: e.tensor_scalar(
                        rows[:, i, 0:D], x_res[:, i, :], mean_var[:, i, 0:1], rstd[:, 0, i:i + 1],
                        ALU.subtract, ALU.mult), [rs, *rows_free], s_norm))
                for i0 in range(a, b, 4):
                    for k in range(KD):
                        n = (i0 // 4) * KD + k
                        bk = n % 4
                        for i in range(i0, i0 + 4):
                            tr = put("tensor", lambda e, i=i, k=k, bk=bk, i0=i0: e.transpose(
                                bank[bk][:, (i - i0) * P:(i - i0 + 1) * P], rows[:, i, k * P:(k + 1) * P],
                                ident[:, :]), [normed[i], consts_done, *free[bk]], s_tr)
                        if n % 2:
                            mk = put("vector", lambda e, k=k, bk=bk, i0=i0: e.tensor_copy(
                                feat[:, k, i0 * P:(i0 + 4) * P], bank[bk][:, :]), [tr, *feat_free], s_feat_v)
                        else:
                            mk = put("scalar", lambda e, k=k, bk=bk, i0=i0: e.activation(
                                feat[:, k, i0 * P:(i0 + 4) * P], bank[bk][:, :], ACT.Copy), [tr, *feat_free],
                                s_feat_a)
                        free[bk] = (mk,)
                        feat_marks.append(mk)
            return normed, feat_marks

        fat = [0]

        def fcarve(n):
            fat[0] += n
            return feat[:, 1, fat[0] - n:fat[0]]

        logits = fcarve(NT * E).rearrange("p (i e) -> p i e", e=E)
        probs = fcarve(NT * E).rearrange("p (i e) -> p i e", e=E)
        scratch = fcarve(4 * NT * E).rearrange("p (n i e) -> p n i e", n=4, e=E)
        sel = fcarve(TOP * NT * E).rearrange("p (n i e) -> p n i e", n=TOP, e=E)
        chosen = fcarve(NT * E).rearrange("p (i e) -> p i e", e=E)
        chosen_bf = sb("chosen_bf", [P, NT, E], BF16)
        small = sb("small", [P, 12, NT])
        per_expert = sb("per_expert", [P, 12, E])
        slot_no = sb("slot_no", [P, TOP, NT], U32)
        steps_gt = fcarve(E * S // TILE).rearrange("p (e t) -> p e t", e=E)
        tile_cmp = fcarve(N_TILES * E).rearrange("p (j e) -> p j e", e=E)
        tile_mask = fcarve(N_TILES * E).rearrange("p (j e) -> p j e", e=E)
        tile_exp = sb("tile_exp", [P, N_TILES])
        tile_exp_i = sb("tile_exp_i", [P, N_TILES], I32)
        tile_hot = sb("tile_hot", [P, 3, E])
        v_part = sb("v_part", [P, KD, N_TILES])
        v_rows = sb("v_rows", [P, D])
        v_half = sb("v_half", [P, D])
        s_gate, s_dve, s_gexp, s_ared = sig("gate_mm"), sig("routing"), sig("gate_exp"), sig("all_reduce")
        s_cnt, s_scat = sig("count_mm"), sig("scattered")
        s_cht, s_chc = sig("chosen_tr"), sig("chosen_copy")
        s_slot = [sig(f"slot_tile{i}") for i in range(3)]
        s_stage, s_xt, s_xtc, s_wb, s_wbt, s_wbc = (sig("staged"), sig("tile_tr"), sig("tile_copied"),
                                                     sig("weight_col"), sig("weight_tr"), sig("weight_row"))
        s_mm = [sig(f"layer_mm{l}") for l in range(LAYERS)]
        s_act_a, s_act_v = sig("relu_by_scalar"), sig("relu_by_vector")
        s_wy, s_vp = sig("weighted"), sig("v_partial")
        s_vt, s_vr, s_vm, s_vh, s_cmb, s_xadd = (sig("v_tr"), sig("v_rows"), sig("v_mm"), sig("v_half"),
                                                 sig("combine"), sig("x_added"))

        at = [0]

        def carve(n):
            at[0] += n
            assert at[0] <= WORK
            return work[:, at[0] - n:at[0]]

        NXG = 3
        W_RING = LAYERS + 1
        x_slot = carve(NXG * TS * ROW).rearrange("p (b u r) -> p b u r", b=NXG, u=TS)
        staged = carve(2 * LAYERS * WROW).rearrange("p (b l w) -> p b l w", b=2, l=LAYERS)
        acts = carve(3 * 2 * KD * TILE).rearrange("p (l b k s) -> p l b k s", l=3, b=2, k=KD)
        weighted = carve(2 * KD * TILE).rearrange("p (b m s) -> p b m s", b=2, m=KD)
        w_row = carve(W_RING * TILE).rearrange("p (b s) -> p b s", b=W_RING)
        w_wide = carve(2 * TS * P).rearrange("p (b u s) -> p b u s", b=2, u=TS)
        w_pick = carve(2 * TS * E).rearrange("p (b u e) -> p b u e", b=2, u=TS)
        w_col = carve(2 * TS).rearrange("p (b u) -> p b u", b=2)

        def bc(ap, axis, shape):
            return ap.unsqueeze(axis).to_broadcast(shape)

        def moe(f, x_ready, experts_loaded, work_free, rows_free, feat_free):
            normed, feat_marks = layer_norm(x_ready, rows_free, feat_free)
            PNE = [P, NT, E]

            gate_bank = bank[4]
            for i in range(NT):
                for k in range(KD):
                    g_mm = put("tensor", lambda e, i=i, k=k: e.matmul(
                        gate_bank[:, i * E:(i + 1) * E], feat[:, k, i * P:(i + 1) * P], gate_w_sb[:, k, :],
                        start=(k == 0), stop=(k == KD - 1)),
                        [small_loaded, *feat_marks[(i // 4) * KD:(i // 4) * KD + KD], *free[4]], s_gate)
            v_last = [None]

            def v(emit, *waits):
                v_last[0] = put("vector", emit, [v_last[0], *waits], s_dve)
                return v_last[0]

            gate_v = gate_bank[:, 0:NT * E].rearrange("p (i e) -> p i e", e=E)
            v(lambda e: e.tensor_tensor(logits[:, :, :], gate_v, bc(gate_b_sb[:, :], 1, PNE), ALU.add), g_mm)
            free[4] = (v_last[0],)
            pe = lambda n: per_expert[:, n, :]
            m = v(lambda e: e.tensor_reduce(pe(0), logits[:, :, :].rearrange("p i e -> p e i"), AX_X, ALU.max))
            m = put("gpsimd", lambda e: e.partition_all_reduce(pe(1), pe(0), P, REDUCE.max), [m], s_ared)
            m = v(lambda e: e.tensor_tensor(logits[:, :, :], logits[:, :, :], bc(pe(1), 1, PNE), ALU.subtract), m)
            m = put("scalar", lambda e: e.activation(probs[:, :, :], logits[:, :, :], ACT.Exp), [m], s_gexp)
            m = v(lambda e: e.tensor_reduce(pe(2), probs[:, :, :].rearrange("p i e -> p e i"), AX_X, ALU.add), m)
            m = put("gpsimd", lambda e: e.partition_all_reduce(pe(3), pe(2), P, REDUCE.add), [m], s_ared)
            v(lambda e: e.reciprocal(pe(4), pe(3)), m)
            v(lambda e: e.tensor_tensor(probs[:, :, :], probs[:, :, :], bc(pe(4), 1, PNE), ALU.mult))

            left = probs
            for c in range(TOP):
                top, rank = small[:, 2 * c, :], small[:, 2 * c + 1, :]
                v(lambda e, left=left, top=top: e.tensor_reduce(top, left[:, :, :], AX_X, ALU.max))
                v(lambda e, left=left, top=top: e.tensor_tensor(scratch[:, 0], left[:, :, :], bc(top, 2, PNE),
                                                                ALU.is_equal))
                v(lambda e: e.tensor_tensor(scratch[:, 1], scratch[:, 0], bc(expert_rank[:, :], 1, PNE), ALU.mult),
                  consts_done)
                v(lambda e, rank=rank: e.tensor_reduce(rank, scratch[:, 1], AX_X, ALU.max))
                v(lambda e, c=c, rank=rank: e.tensor_tensor(sel[:, c], scratch[:, 1], bc(rank, 2, PNE), ALU.is_equal))
                if c == 0:
                    v(lambda e: e.scalar_tensor_tensor(scratch[:, 2], sel[:, 0], -4.0, probs[:, :, :],
                                                       ALU.mult, ALU.add))
                    left = scratch[:, 2]
            v(lambda e: e.tensor_tensor(chosen[:, :, :], sel[:, 0], sel[:, 1], ALU.add))
            cb = v(lambda e: e.tensor_copy(chosen_bf[:, :, :], chosen[:, :, :]))
            w_done = v(lambda e: e.tensor_tensor(rows[:, :, D:ROW], chosen[:, :, :], probs[:, :, :], ALU.mult))

            flat = chosen_bf[:, :, :].rearrange("p i e -> p (i e)")
            put("tensor", lambda e: e.matmul(bank[5][:, 0:NT * E], before[:, :], flat, start=True, stop=True),
                [cb, *free[5]], s_cnt)
            cnt = put("tensor", lambda e: e.matmul(bank[6][:, 0:NT * E], ones_bf[:, :], flat, start=True,
                                                   stop=True), [*free[6]], s_cnt)
            for i0 in range(0, NT, 4):
                bk = (i0 // 4) % 2
                for i in range(i0, i0 + 4):
                    t = put("tensor", lambda e, i=i, i0=i0, bk=bk: e.transpose(
                        bank[bk][0:E, (i - i0) * P:(i - i0 + 1) * P], chosen[:, i, :], ident[:, :]),
                        [*free[bk]], s_cht)
                cp = put("scalar", lambda e, i0=i0, bk=bk: e.activation(
                    feat[0:E, 0, i0 * P:(i0 + 4) * P], bank[bk][0:E, :], ACT.Copy), [t, g_mm], s_chc)
                free[bk] = (cp,)
            chosen_t_done = cp

            em = scratch[:, 0].rearrange("p i e -> p (i e)").rearrange("p (e i) -> p e i", e=E)
            run = scratch[:, 1].rearrange("p i e -> p (i e)").rearrange("p (e i) -> p e i", e=E)
            prior = scratch[:, 2].rearrange("p i e -> p (i e)").rearrange("p (e i) -> p e i", e=E)
            v(lambda e: e.tensor_copy(em, bank[6][:, 0:NT * E].rearrange("p (i e) -> p e i", e=E)), cnt)
            free[6] = (v_last[0],)
            fl = lambda ap: ap.rearrange("p e i -> p (e i)")
            v(lambda e: e.tensor_tensor_scan(fl(run), fl(carry[:, :, :]), fl(em), 0.0, ALU.mult, ALU.add))
            v(lambda e: e.tensor_tensor(prior, run, em, ALU.subtract))
            SE = [P, E, S // TILE]
            v(lambda e: e.tensor_tensor(steps_gt[:, :, :], run[:, :, NT - 1:NT].to_broadcast(SE),
                                        bc(tile_steps[:, :], 1, SE), ALU.is_gt))
            v(lambda e: e.tensor_reduce(pe(5), steps_gt[:, :, :], AX_X, ALU.add))
            v(lambda e: e.tensor_tensor_scan(pe(6), ones_e[:, :], pe(5), 0.0, ALU.mult, ALU.add))
            v(lambda e: e.tensor_tensor(pe(7), pe(6), pe(5), ALU.subtract))
            v(lambda e: e.tensor_scalar(pe(8), pe(7), float(TILE), None, ALU.mult))
            v(lambda e: e.tensor_tensor(scratch[:, 3], bank[5][:, 0:NT * E].rearrange("p (i e) -> p i e", e=E),
                                        prior.rearrange("p e i -> p i e"), ALU.add))
            free[5] = (v_last[0],)
            v(lambda e: e.tensor_tensor(scratch[:, 3], scratch[:, 3], bc(pe(8), 1, PNE), ALU.add))
            slot_marks = []
            for c in range(TOP):
                v(lambda e, c=c: e.tensor_tensor(scratch[:, 0], sel[:, c], scratch[:, 3], ALU.mult))
                v(lambda e, c=c: e.tensor_reduce(small[:, 4 + c, :], scratch[:, 0], AX_X, ALU.add))
                slot_marks.append(v(lambda e, c=c: e.tensor_copy(slot_no[:, c, :], small[:, 4 + c, :])))
            TE = [P, N_TILES, E]
            v(lambda e: e.tensor_tensor(tile_cmp[:, :, :], bc(tile_ids[:, :], 2, TE), bc(pe(6), 1, TE), ALU.is_ge))
            v(lambda e: e.tensor_reduce(tile_exp[:, :], tile_cmp[:, :, :], AX_X, ALU.add))
            v(lambda e: e.tensor_scalar(tile_exp[:, :], tile_exp[:, :], float(E - 1), None, ALU.min))
            table = v(lambda e: e.tensor_copy(tile_exp_i[:, :], tile_exp[:, :]))
            masks = v(lambda e: e.tensor_tensor(tile_mask[:, :, :], bc(tile_exp[:, :], 2, TE),
                                                bc(expert_ids[:, :], 1, TE), ALU.is_equal))
            v(lambda e: e.tensor_scalar(tile_hot[:, 0, :], pe(7), tile_col[:, 0:1], None, ALU.is_le))
            v(lambda e: e.tensor_scalar(tile_hot[:, 1, :], pe(6), tile_col[:, 0:1], None, ALU.is_le))
            hot = v(lambda e: e.tensor_tensor(tile_hot[:, 2, :], tile_hot[:, 0, :], tile_hot[:, 1, :], ALU.subtract))

            for c in range(TOP):
                for i in range(NT):
                    scattered = put("gpsimd", lambda e, c=c, i=i: e.indirect_dma_start(
                        out=slots[f], out_offset=bass.IndirectOffsetOnAxis(ap=slot_no[:, c, i:i + 1], axis=0),
                        in_=rows[:, i, :], in_offset=None), [slot_marks[c], w_done, slots_zeroed[f]], s_scat, 16)

            xs = slots[f].rearrange("(j u p) r -> j p u r", u=TS, p=P)
            loaded, xt_done, xt_copied, w_ready = {}, {}, {}, {}
            stage_done = {(l, b): () for l in range(LAYERS) for b in range(2)}
            staged_marks, layer_marks, relu_marks = {}, {}, {}
            x_free = {}
            wy_marks, vp_marks, wide_read, widened = {}, {}, {}, {}

            def stage(j, l):
                if not 0 <= j < N_TILES:
                    return

                def emit(e):
                    expert = e.value_load(tile_exp_i[0:1, j:j + 1], min_val=0, max_val=E - 1)
                    return e.tensor_copy(staged[:, j % 2, l, :],
                                         experts[:, bass.ds(expert, 1), l, :].rearrange("p a w -> p (a w)"))
                staged_marks[j, l] = put("vector", emit, [
                    table, experts_loaded, *work_free, layer_marks.get((j - 2, l)),
                    *relu_marks.get((j - 2, l), ())], s_stage)

            def load(j):
                if j >= N_TILES:
                    return
                loaded[j] = dma("sync", x_slot[:, j % NXG], xs[j], [scattered, *work_free, *x_free.get(j - NXG, ())],
                                s_slot[j % NXG])

            def widen_weight(j):
                if j >= N_TILES:
                    return
                b = j % 2
                pk = put("vector", lambda e: e.tensor_tensor(
                    w_pick[:, b], x_slot[:, j % NXG, :, D:ROW], bc(tile_mask[:, j, :], 1, [P, TS, E]), ALU.mult),
                    [loaded[j], masks, *work_free], s_wb)
                pk = put("vector", lambda e: e.tensor_reduce(w_col[:, b], w_pick[:, b], AX_X, ALU.add), [pk], s_wb)
                widened[j] = put("vector", lambda e: e.tensor_copy(w_wide[:, b], bc(w_col[:, b], 2, [P, TS, P])),
                                 [pk, wide_read.get(j - 2)], s_wb)

            def transpose_weight(j):
                if j >= N_TILES:
                    return
                for u in range(TS):
                    wt = put("tensor", lambda e, u=u: e.transpose(
                        bank[1][:, u * P:(u + 1) * P], w_wide[:, j % 2, u], ident[:, :]), [widened[j], *free[1]], s_wbt)
                wide_read[j] = wt
                w_ready[j] = put("scalar", lambda e: e.activation(w_row[:, j % W_RING], bank[1][:, 0:TILE], ACT.Copy),
                                 [wt, *wy_marks.get(j - W_RING, ()), *work_free], s_wbc)
                free[1] = (w_ready[j],)

            def transpose_tile(j):
                if j >= N_TILES:
                    return
                b = j % 2
                for u in range(TS):
                    for k in range(KD):
                        xt_done[j] = put("tensor", lambda e, u=u, k=k: e.transpose(
                            bank[0][:, k * TILE + u * P:k * TILE + (u + 1) * P],
                            x_slot[:, j % NXG, u, k * P:(k + 1) * P], ident[:, :]), [loaded[j], *free[0]], s_xt)
                x_free[j] = (xt_done[j], widened[j])
                xt_copied[j] = put("scalar", lambda e: e.activation(
                    acts[:, 0, b].rearrange("p k s -> p (k s)"), bank[0][:, :], ACT.Copy),
                    [xt_done[j], layer_marks.get((j - 2, 0)), *work_free], s_xtc)
                free[0] = (xt_copied[j],)

            def layer(j, l):
                if not 0 <= j < N_TILES:
                    return
                b = j % 2
                src = (xt_copied[j],) if l == 0 else relu_marks[j, l - 1]
                bk = 2 + l
                for m in range(KD):
                    for k in range(KD):
                        mm = put("tensor", lambda e, m=m, k=k: e.matmul(
                            bank[bk][:, m * TILE:(m + 1) * TILE],
                            staged[:, b, l, k * D + m * P:k * D + (m + 1) * P], acts[:, l, b, k],
                            start=(k == 0), stop=(k == KD - 1)),
                            [staged_marks[j, l], *src, *free[bk]], s_mm[l] if m == k == KD - 1 else None)
                layer_marks[j, l] = mm
                bias = lambda m: staged[:, b, l, KD * D + m:KD * D + m + 1]
                psum = lambda m: bank[bk][:, m * TILE:(m + 1) * TILE]
                if l < LAYERS - 1:
                    dst_free = layer_marks.get((j - 2, l + 1))
                    for m in range(KD):
                        if l == 0:
                            relu = put("scalar", lambda e, m=m: e.activation(
                                acts[:, l + 1, b, m], psum(m), ACT.Relu, bias=bias(m)), [mm, dst_free], s_act_a)
                        else:
                            relu = put("vector", lambda e, m=m: e.tensor_scalar(
                                acts[:, l + 1, b, m], psum(m), bias(m), 0.0, ALU.add, ALU.max), [mm, dst_free], s_act_v)
                    relu_marks[j, l] = (relu,)
                    free[bk] = (relu,)
                else:
                    for m in range(KD):
                        wy = put("vector", lambda e, m=m: e.scalar_tensor_tensor(
                            weighted[:, b, m], psum(m), bias(m), w_row[:, j % W_RING], ALU.add, ALU.mult),
                            [mm, w_ready[j], *vp_marks.get(j - 2, ())], s_wy)
                        vp = put("scalar", lambda e, m=m: e.activation(
                            weighted[:, b, m], weighted[:, b, m], ACT.Relu, accum_out=v_part[:, m, j:j + 1]),
                            [wy], s_vp)
                    free[bk] = (wy,)
                    relu_marks[j, l] = (wy,)
                    wy_marks[j] = (wy,)
                    vp_marks[j] = (vp,)

            load(0)
            load(1)
            stage(0, 0)
            for j in range(N_TILES + LAYERS):
                load(j + 2)
                widen_weight(j)
                layer(j - 3, 2)
                stage(j - 1, 2)
                transpose_tile(j)
                layer(j - 2, 1)
                stage(j, 1)
                transpose_weight(j)
                layer(j - 1, 0)
                stage(j + 1, 0)
            work_done = [layer_marks[N_TILES - 1, 2], *wy_marks[N_TILES - 1], *vp_marks[N_TILES - 1],
                         staged_marks[N_TILES - 1, LAYERS - 1]]

            for m in range(KD):
                t = put("tensor", lambda e, m=m: e.transpose(bank[5][0:N_TILES, m * P:(m + 1) * P],
                                                             v_part[:, m, :], ident[:, :]),
                        [*vp_marks[N_TILES - 1], *free[5]], s_vt)
            c = put("vector", lambda e: e.tensor_copy(v_rows[0:N_TILES, :], bank[5][0:N_TILES, 0:D]), [t], s_vr)
            free[5] = (c,)
            t = put("tensor", lambda e: e.matmul(bank[6][0:E, 0:D], tile_hot[0:N_TILES, 2, :], v_rows[0:N_TILES, :],
                                                 start=True, stop=True), [c, hot, *free[6]], s_vm)
            vh = put("vector", lambda e: e.tensor_scalar(v_half[0:E, :], bank[6][0:E, 0:D], 0.5, None, ALU.mult),
                     [t], s_vh)
            free[6] = (vh,)
            x_marks = []
            for i0 in range(0, NT, 2):
                bk = (i0 // 2) % 3 if True else 0
                for i in (i0, i0 + 1):
                    cm = put("tensor", lambda e, i=i, i0=i0, bk=bk: e.matmul(
                        bank[bk][:, (i - i0) * D:(i - i0 + 1) * D], feat[0:E, 0, i * P:(i + 1) * P], v_half[0:E, :],
                        start=True, stop=True), [vh, chosen_t_done, *free[bk]], s_cmb)
                xm = put("vector", lambda e, i0=i0, bk=bk: e.tensor_tensor(
                    x_res[:, i0:i0 + 2, :], x_res[:, i0:i0 + 2, :],
                    bank[bk][:, :].rearrange("p (a d) -> p a d", a=2), ALU.add), [cm], s_xadd)
                free[bk] = (xm,)
                x_marks += [xm, xm]
            return dict(x=x_marks, work=work_done, rows=[scattered], feat=[cm], phase=[staged_marks[N_TILES - 1, 2]])

        def attention(x_ready, work_free, phase_free, rows_free, feat_free):
            at[0] = 0
            bf = lambda ap: ap.bitcast(BF16)
            stack = bf(carve(2 * 2 * S // 2)).rearrange("p (b c s) -> p b c s", b=2, c=2)
            maxima = carve(2 * NJ * TPJ * (NJ + 1)).rearrange("p (b j i c) -> p b j i c", b=2, j=NJ, i=TPJ)
            neg_max = carve(4 * TPJ).rearrange("p (b i) -> p b i", b=4)
            max_parts = bf(carve(4 * TPJ * M_PARTS // 2)).rearrange("p (b i m) -> p b i m", b=4, i=TPJ)
            recip = carve(2 * TPJ).rearrange("p (b i) -> p b i", b=2)
            p_ring = feat[:, 0, :].rearrange("p (r s) -> p r s", r=P_RING)
            acc_sb = feat[:, 1, 0:2 * QB].rearrange("p (b s) -> p b s", b=2)
            head_sum = feat[:, 1, 2 * QB:2 * QB + 2 * TPJ * VW].rearrange("p (b i w) -> p b i w", b=2, i=TPJ)
            flat_rows = rows[:, :, :].rearrange("p i r -> p (i r)")
            split_bf = bf(flat_rows[:, 0:SPLIT * 3 * QB // 2]).rearrange("p (b t s) -> p b t s", b=SPLIT, t=3)
            split_f = flat_rows[:, SPLIT * 3 * QB // 2:SPLIT * 5 * QB // 2].rearrange("p (b s) -> p b s", b=SPLIT)
            heads = rows[:, :, 0:D]

            normed, feat_marks = layer_norm(x_ready, rows_free, feat_free)

            rows_read = (s_tr, s_tr.count)
            s_pm, s_p1, s_r1, s_p2, s_p3 = (sig("proj_mm"), sig("part1"), sig("rest1"), sig("part2"), sig("part3"))
            s_wr = [sig(f"parts_stored{i}") for i in range(SPLIT)]
            parts_stored = {}
            store = {}
            p3m, r1m = {}, {}

            def project_chunk(ob, sc):
                n = len(store)
                bk, b = n % 4, n % SPLIT
                for k in range(KD):
                    mm = put("tensor", lambda e, k=k: e.matmul(
                        bank[bk][:, :], w_qkv_sb[:, k, ob * P:(ob + 1) * P], feat[:, k, sc * QB:(sc + 1) * QB],
                        start=(k == 0), stop=(k == KD - 1)),
                        [attw_loaded, *feat_marks[sc * KD:(sc + 1) * KD], *free[bk]], s_pm)
                p1 = put("scalar", lambda e: e.activation(split_bf[:, b, 0], bank[bk][:, :], ACT.Copy),
                         [mm, store.get(n - SPLIT), rows_read], s_p1)
                r1 = put("vector", lambda e: e.tensor_tensor(split_f[:, b], bank[bk][:, :], split_bf[:, b, 0],
                                                             ALU.subtract),
                         [p1, p3m.get(n - SPLIT), rows_read], s_r1)
                free[bk] = (r1,)
                p2 = put("scalar", lambda e: e.activation(split_bf[:, b, 1], split_f[:, b], ACT.Copy), [r1], s_p2)
                p3m[n] = put("gpsimd", lambda e: e.tensor_tensor(split_bf[:, b, 2], split_f[:, b],
                                                                 split_bf[:, b, 1], ALU.subtract),
                             [p2, store.get(n - SPLIT)], s_p3)
                qk, r0 = ob // KD, (ob % KD) * P
                store[n] = dma("sync", parts_dram[qk, :, r0:r0 + P, sc * QB:(sc + 1) * QB]
                               .rearrange("t r s -> r t s"), split_bf[:, b], [p3m[n], p1, p2], s_wr[b])

            def project(ob):
                for sc in range(NJ):
                    project_chunk(ob, sc)
                n = len(store)
                parts_stored[ob] = tuple(store[n - 1 - i] for i in range(SPLIT))

            s_stack = [sig(f"stack{i}") for i in range(2)]
            stack_loaded = {}
            b_last = {}

            def load_stack(h):
                half = h // (H // KD)
                waits = [*parts_stored[half], *parts_stored[KD + half], *work_free,
                         b_last.get(h - 2)]
                for r, pair in enumerate(PARTS):
                    for c in range(2):
                        stack_loaded[h] = dma("sync", stack[r * HD:(r + 1) * HD, h % 2, c, :],
                                              parts_dram[c, pair[c], h * HD:(h + 1) * HD, :], waits, s_stack[h % 2])

            project(0)
            project(KD)
            load_stack(0)
            load_stack(1)

            s_vmm, s_vcp, s_ones = sig("v_mm_"), sig("v_copied"), sig("ones_set")
            put("vector", lambda e: e.memset(v_aug[:, :, :, HD:VW], 1.0), [*phase_free], s_ones)
            for b in range(2):
                ones_set = put("vector", lambda e, b=b: e.memset(
                    stack[QK_ROWS:QK_ROWS + M_PARTS, b, 1, :], 1.0), [*work_free], s_ones)
            for i in range(NT):
                bk = 4 + i % 2
                for k in range(KD):
                    mm = put("tensor", lambda e, k=k, i=i, bk=bk: e.matmul(
                        bank[bk][:, 0:D], feat[:, k, i * P:(i + 1) * P], w_qkv_sb[:, k, 2 * D:3 * D],
                        start=(k == 0), stop=(k == KD - 1)), [*free[bk]], s_vmm)
                v_copied = put("scalar", lambda e, i=i, bk=bk: e.activation(
                    v_aug[:, i, :, 0:HD], bank[bk][:, 0:D].rearrange("p (h d) -> p h d", h=H), ACT.Copy),
                    [mm, *phase_free], s_vcp)
                free[bk] = (v_copied,)
            project(1)
            project(KD + 1)
            store_done = parts_stored[KD + 1]
            feat_read = (s_pm, s_pm.count)

            s_s, s_e, s_pv, s_acc, s_sum, s_rl, s_head = (sig("scores_t"), sig("exp"), sig("pv"), sig("acc_copied"),
                                                          sig("quads_summed"), sig("recip"), sig("head_out"))
            s_a, s_mx, s_neg, s_mp, s_mt, s_mrow = (sig("scores"), sig("max_part"), sig("neg_max"),
                                                    sig("max_parts"), sig("max_tr"), sig("max_row"))
            put("tensor", lambda e: e.matmul(bank[ACC_BANK][:, :], zeros_bf[:, 0:P], zeros_bf[:, :], start=True,
                                             stop=True), [*free[ACC_BANK]], s_pv)
            mx_set = put("vector", lambda e: e.memset(maxima, NEG), [*work_free], s_ones)

            units = [(h, j) for h in range(H) for j in range(NJ)]
            a_items = [(h, j, i, c) for h, j in units for i in range(TPJ) for c in range(j + 1)]
            b_items = [(h, j, t) for h, j in units for t in range(TPJ * (j + 1))]
            assert len(a_items) == len(b_items)
            mrow_done, neg_done, p_marks, exp_marks, pv_marks, mp_marks = {}, {}, {}, {}, {}, {}

            def a_item(n):
                h, j, i, c = a_items[n]
                bk = A_BANKS[n % len(A_BANKS)]
                w = QB if c < j else (i + 1) * P
                q0 = (TPJ * j + i) * P
                mm = put("tensor", lambda e: e.matmul(
                    bank[bk][:, 0:w], stack[0:QK_ROWS, h % 2, 0, q0:q0 + P], stack[0:QK_ROWS, h % 2, 1, c * QB:c * QB + w],
                    start=True, stop=True), [stack_loaded[h], *free[bk]], s_a)
                col = lambda k: maxima[:, h % 2, j, i, k:k + 1]
                last = None
                prev = neg_done.get((h - 2, j))
                full = w if c < j else w - P
                if full:
                    last = put("vector", lambda e: e.tensor_reduce(col(c if c < j else NJ), bank[bk][:, 0:full], AX_X, ALU.max),
                               [mm, mx_set, prev], s_mx)
                if c == j:
                    last = put("vector", lambda e: e.tensor_tensor_reduce(
                        bank[bk][:, w - P:w], bank[bk][:, w - P:w], mask_s[:, :], 1.0, NEG, ALU.add, ALU.max,
                        col(c)), [mm, mx_set, prev, consts_done], s_mx)
                free[bk] = (last,)
                if i == TPJ - 1 and c == j:
                    u = h * NJ + j
                    neg_done[h, j] = put("vector", lambda e: e.tensor_reduce(
                        neg_max[:, u % 4, :], maxima[:, h % 2, j], AX_X, ALU.max, negate=True),
                        [last, mp_marks.get(u - 4)], s_neg)
                    m1 = put("gpsimd", lambda e: e.tensor_copy(max_parts[:, u % 4, :, 0], neg_max[:, u % 4, :]),
                             [neg_done[h, j], mt_marks.get(u - 4)], s_mp)
                    mp_marks[u] = put("gpsimd", lambda e: e.tensor_tensor(
                        max_parts[:, u % 4, :, 1], neg_max[:, u % 4, :], max_parts[:, u % 4, :, 0], ALU.subtract),
                        [m1], s_mp)
                    return u
                return None

            mt_marks = {}

            def max_row(u):
                h, j = units[u]
                for i in range(TPJ):
                    mt_marks[u] = put("tensor", lambda e, i=i: e.matmul(
                        bank[M_BANK][QK_ROWS:QK_ROWS + M_PARTS, i * P:(i + 1) * P], max_parts[:, u % 4, i, :],
                        ident_bf[:, :], start=True, stop=True), [mp_marks[u], *free[M_BANK]], s_mt)
                mrow_done[u] = put("scalar", lambda e: e.activation(
                    stack[QK_ROWS:QK_ROWS + M_PARTS, h % 2, 0, j * QB:(j + 1) * QB],
                    bank[M_BANK][QK_ROWS:QK_ROWS + M_PARTS, :], ACT.Copy), [mt_marks[u], b_last.get(h - 2)], s_mrow)
                free[M_BANK] = (mrow_done[u],)

            def b_item(n):
                h, j, t = b_items[n]
                u = h * NJ + j
                bk = S_BANKS[n % len(S_BANKS)]
                diag = t - TPJ * j
                lo = max(diag, 0) * P
                mm = put("tensor", lambda e: e.matmul(
                    bank[bk][:, lo:QB], stack[0:QK_ROWS + M_PARTS, h % 2, 1, t * P:(t + 1) * P],
                    stack[0:QK_ROWS + M_PARTS, h % 2, 0, j * QB + lo:(j + 1) * QB], start=True, stop=(diag < 0)),
                    [mrow_done[u], stack_loaded[h], ones_set, *free[bk]], s_s)
                if diag >= 0:
                    mm = put("tensor", lambda e: e.matmul(bank[bk][:, lo:lo + P], ident_bf[:, :], mask_t[:, :],
                                                          start=False, stop=True), [], s_s)
                b_last[h] = mm
                exp_marks[n] = put("scalar", lambda e: e.activation(
                    p_ring[:, n % P_RING, lo:QB], bank[bk][:, lo:QB], ACT.Exp, scale=HD ** -0.5),
                    [mm, pv_marks.get(n - P_RING), feat_read], s_e)
                free[bk] = (exp_marks[n],)

            def pv_group(n0, half):
                h, j, t0 = b_items[n0]
                u = h * NJ + j
                first = t0 == 0
                zero_start = first and j == 0
                if zero_start and half == 0:
                    for c in range(TPJ):
                        put("tensor", lambda e, c=c: e.matmul(
                            bank[ACC_BANK][32 * c:32 * c + VW, :], zeros_bf[:, 0:VW], zeros_bf[:, :],
                            start=True, stop=False), [*free[ACC_BANK]], s_pv)
                for c in range(TPJ):
                    t = t0 + c
                    lo, hi = max((t - TPJ * j) * P, half * QB // 2), (half + 1) * QB // 2
                    if lo >= hi:
                        continue
                    mark = put("tensor", lambda e, c=c, t=t, lo=lo, hi=hi: e.matmul(
                        bank[ACC_BANK][32 * c:32 * c + VW, lo:hi], v_aug[:, t, h, :], p_ring[:, (n0 + c) % P_RING, lo:hi],
                        start=(first and not zero_start and half == 0), stop=(t0 == TPJ * j and half == 1)),
                        [exp_marks[n0 + c], v_copied, ones_set, *free[ACC_BANK]], s_pv)
                    if half:
                        pv_marks[n0 + c] = mark
                if t0 == TPJ * j and half:
                    cp = put("scalar", lambda e: e.activation(acc_sb[:, u % 2, :], bank[ACC_BANK][:, :], ACT.Copy),
                             [pv_marks[n0 + TPJ - 1], sum_marks.get(u - 2), feat_read], s_acc)
                    free[ACC_BANK] = (cp,)
                    return u, cp
                return None

            sum_marks = {}
            s_hs = sig("head_sum")
            head_marks = []

            def finish_unit(u, cp):
                h, j = units[u]
                for i in range(TPJ):
                    sum_marks[u] = put("tensor", lambda e, i=i: e.transpose(
                        bank[O_BANK][:, i * P:(i + 1) * P], acc_sb[:, u % 2, i * P:(i + 1) * P], ident[:, :]),
                        [cp, *free[O_BANK]], s_sum)
                o = bank[O_BANK][:, :].rearrange("p (i c w) -> p i w c", i=TPJ, c=TPJ)
                hs = put("vector", lambda e: e.tensor_reduce(head_sum[:, u % 2], o[:, :, 0:VW, :], AX_X, ALU.add),
                         [sum_marks[u], head_marks[-2] if u >= 2 else None], s_hs)
                free[O_BANK] = (hs,)
                rl = put("vector", lambda e: e.reciprocal(recip[:, u % 2, :], head_sum[:, u % 2, :, HD]), [hs], s_rl)
                hm = put("vector", lambda e: e.tensor_tensor(
                    heads[:, TPJ * j:TPJ * (j + 1), h * HD:(h + 1) * HD], head_sum[:, u % 2, :, 0:HD],
                    bc(recip[:, u % 2, :], 2, [P, TPJ, HD]), ALU.mult), [rl, *store_done], s_head)
                head_marks.append(hm)

            due = {}
            total = len(a_items)
            unfinished = []
            for n in range(total + LEAD):
                if n < total:
                    u = a_item(n)
                    if u is not None:
                        due.setdefault(n + 5, []).append(u)
                for u in due.pop(n, []):
                    max_row(u)
                bn = n - LEAD
                if bn >= 0:
                    h, j, t = b_items[bn]
                    if j == 2 and t == 0 and 1 <= h < H - 1:
                        load_stack(h + 1)
                    b_item(bn)
                    group = bn - bn % TPJ
                    if bn % TPJ == 1 and group:
                        pv_group(group - TPJ, 0)
                    if bn % TPJ == 2 and unfinished:
                        finish_unit(*unfinished.pop())
                    if bn % TPJ == 3 and group:
                        done = pv_group(group - TPJ, 1)
                        if done:
                            unfinished.append(done)
            for u, cp in unfinished:
                finish_unit(u, cp)
            pv_group(total - TPJ, 0)
            finish_unit(*pv_group(total - TPJ, 1))
            all_heads = head_marks[-1]
            last_pv = pv_marks[total - 1]

            s_ht, s_hc, s_hcv, s_om, s_xo = (sig("heads_tr"), sig("heads_copied"), sig("heads_copied_v"),
                                             sig("out_mm"), sig("x_attended"))
            x_marks = []
            for i0 in range(0, NT, 4):
                cps = []
                for k in range(KD):
                    bk = ((i0 // 4) * KD + k) % 4
                    for i in range(i0, i0 + 4):
                        tr = put("tensor", lambda e, i=i, k=k, bk=bk, i0=i0: e.transpose(
                            bank[bk][:, (i - i0) * P:(i - i0 + 1) * P], rows[:, i, k * P:(k + 1) * P], ident[:, :]),
                            [all_heads, *free[bk]], s_ht)
                    if k:
                        cp = put("vector", lambda e, k=k, bk=bk, i0=i0: e.tensor_copy(
                            feat[:, k, i0 * P:(i0 + 4) * P], bank[bk][:, :]), [tr, last_pv, sum_marks[len(units) - 1]], s_hcv)
                    else:
                        cp = put("scalar", lambda e, k=k, bk=bk, i0=i0: e.activation(
                            feat[:, k, i0 * P:(i0 + 4) * P], bank[bk][:, :], ACT.Copy), [tr, last_pv, sum_marks[len(units) - 1]], s_hc)
                    free[bk] = (cp,)
                    cps.append(cp)
                for i2 in range(i0, i0 + 4, 2):
                    bk = 4 + (i2 // 2) % 4
                    for i in (i2, i2 + 1):
                        for k in range(KD):
                            mm = put("tensor", lambda e, i=i, i2=i2, k=k, bk=bk: e.matmul(
                                bank[bk][:, (i - i2) * D:(i - i2 + 1) * D], feat[:, k, i * P:(i + 1) * P],
                                w_out_sb[:, k, :], start=(k == 0), stop=(k == KD - 1)), [*cps, *free[bk]], s_om)
                    xm = put("vector", lambda e, i2=i2, bk=bk: e.tensor_tensor(
                        x_res[:, i2:i2 + 2, :], x_res[:, i2:i2 + 2, :],
                        bank[bk][:, :].rearrange("p (a d) -> p a d", a=2), ALU.add), [mm], s_xo)
                    free[bk] = (xm,)
                    x_marks += [xm, xm]
            return dict(x=x_marks, work=[last_pv], phase=[last_pv], rows=[tr], feat=[mm])


        experts0 = load_experts(0, [])
        zero_slots(0, [])
        x_ready = [[x_loaded[i // GRP]] for i in range(NT)]
        if True:
            r = moe(0, x_ready, experts0, [], [], [])
            zero_slots(1, [r["work"][0]])
            r = attention([[m] for m in r["x"]], r["work"], r["phase"], r["rows"], r["feat"])
            experts1 = load_experts(1, r["phase"])
            r = moe(1, [[m] for m in r["x"]], experts1, r["work"], r["rows"], r["feat"])
        s_out = sig("stored")
        out_t = out.rearrange("(i p) d -> p i d", p=P)
        for g in range(NT // GRP):
            stored = dma("sync", out_t[:, g * GRP:(g + 1) * GRP, :], x_res[:, g * GRP:(g + 1) * GRP, :],
                         [r["x"][(g + 1) * GRP - 1]], s_out)
        q.lists["sync"].append(((stored,), lambda e: e.nop(), None, 0))

        block = ctx.enter_context(nc.Block())

        @block.sync
        def _(eng):
            q.run("sync", eng)

        @block.gpsimd
        def _(eng):
            q.run("gpsimd", eng)

        @block.scalar
        def _(eng):
            q.run("scalar", eng)

        @block.tensor
        def _(eng):
            q.run("tensor", eng)

        @block.vector
        def _(eng):
            q.run("vector", eng)


def kernel(**inputs):
    import numpy as np
    import concourse.bacc as bacc
    from concourse.bass_utils import run_bass_kernel_spmd

    given = {name: np.asarray(a) for name, a in inputs.items()}
    arrays = {
        "x": given["L0_attn_x"].reshape(S, D),
        "w_qkv_t": given["L0_attn_w_qkv"].T,
        "w_out_t": given["L0_attn_w_out"].T,
    }
    for name in ("gate_w", "gate_b", "w1", "w2", "w3"):
        arrays[name] = given["L0_ffn_" + name]
    biases = np.stack([given["L0_ffn_" + name] for name in ("b1", "b2", "b3")], axis=1)
    arrays["bias_cols"] = biases.reshape(E, LAYERS, KD, P).transpose(3, 0, 1, 2)
    arrays = {name: np.ascontiguousarray(a) for name, a in arrays.items()}
    nc = bacc.Bacc("TRN2", target_bir_lowering=False, num_devices=1)
    args = [nc.dram_tensor("in_" + name, a.shape, F32, kind="ExternalInput").ap() for name, a in arrays.items()]
    out = nc.dram_tensor("out", (S, D), F32, kind="ExternalOutput").ap()
    macaron_block(nc, *args, out)
    r = run_bass_kernel_spmd(nc, [{"in_" + name: a for name, a in arrays.items()}], core_ids=[0])
    return r.results[0]["out"].reshape(1, S, D)
```

```python
from contextlib import ExitStack

import concourse.bass as bass
from concourse import mybir

F32 = mybir.dt.float32
BF16 = mybir.dt.bfloat16
U32 = mybir.dt.uint32
I32 = mybir.dt.int32
ALU = mybir.AluOpType
ACT = mybir.ActivationFunctionType
AX_X = mybir.AxisListType.X
REDUCE = bass.bass_isa.ReduceOp

P = 128
S = 4096
D = 256
NT = S // P
KD = D // P
H = 16
HD = D // H
E = 8
LAYERS = 3
TOP = 2
EPS = 1e-5
NEG = -3.0e38

TILE = 256
TS = TILE // P
CODE_0 = (127 + 7) * P
MAGIC = 1.5 * 2 ** 30
N_TILES = (TOP * S + E * (TILE - 1)) // TILE
N_SUB = N_TILES * TS
ROW = D + E
WROW = KD * D + KD

QB = 512
NJ = S // QB
TPJ = QB // P
K_PARTS = (3, 2, 1)
QK_ROWS = sum(K_PARTS) * HD
M_PARTS = 2
VW = HD + 1
S_BANKS = (0, 1, 2)
A_BANKS = (3, 4, 7)
ACC_BANK, M_BANK, O_BANK = 5, 6, 6
WORK = 10368
P_RING = 8
SPLIT_BF, SPLIT_F = 3, 2
LEAD = 40


class Counter:

    def __init__(self, sem):
        self.sem, self.count = sem, 0


class Queues:

    def __init__(self, nc, ctx):
        self.nc, self.ctx = nc, ctx
        self.lists = {name: [] for name in ("tensor", "vector", "scalar", "gpsimd", "sync")}

    def counter(self, name):
        return Counter(self.ctx.enter_context(self.nc.semaphore(name)))

    def put(self, engine, emit, waits=(), counter=None, amount=1):
        mark = None
        if counter is not None:
            counter.count += amount
            mark = (counter, counter.count)
        self.lists[engine].append((tuple(w for w in waits if w is not None), emit, counter, amount))
        return mark

    def dma(self, engine, out, in_, waits, counter):
        return self.put(engine, lambda e: e.dma_start(out, in_), waits, counter, 16)

    def run(self, engine, eng):
        reached = {}
        for waits, emit, counter, amount in self.lists[engine]:
            for s, value in waits:
                if reached.get(s, 0) < value:
                    eng.wait_ge(s.sem, value)
                    reached[s] = value
            ins = emit(eng)
            if counter is not None:
                ins.then_inc(counter.sem, amount)


def macaron_block(nc, x_in, w_qkv_t, w_out_t, gate_w, gate_b, w1, w2, w3, bias_cols, out):
    with ExitStack() as ctx:
        q = Queues(nc, ctx)
        sig, put, dma = q.counter, q.put, q.dma

        def sb(name, shape, dt=F32):
            return ctx.enter_context(nc.sbuf_tensor(name, shape, dt))

        x_res = sb("x_res", [P, NT, D])
        rows = sb("rows", [P, NT, ROW])
        feat = sb("feat", [P, KD, S])
        phase = sb("phase", [P, E * LAYERS * WROW])
        ident = sb("ident", [P, P])
        ident_bf = sb("ident_bf", [P, P], BF16)
        stats = sb("stats", [P, NT, 6])
        mean_var = sb("mean_var", [P, NT, 2])
        rstd = sb("rstd", [P, 2, NT])
        w_qkv_sb = sb("w_qkv_sb", [P, KD, 3 * D])
        w_out_sb = sb("w_out_sb", [P, KD, D])
        bank = [ctx.enter_context(nc.psum_tensor(f"bank{i}", [P, 512], F32)) for i in range(8)]
        free = {i: () for i in range(8)}

        table = [nc.dram_tensor(f"token_table{f}", (S + 1, ROW), F32).ap() for f in range(2)]
        parts_dram = nc.dram_tensor("qk_parts", (2, 3, D, S), BF16).ap()

        s_const = sig("constants")

        def const(emit):
            last = (s_const, s_const.count) if s_const.count else None
            return put("gpsimd", emit, [last], s_const)

        def diagonal(t, n=P):
            const(lambda e: e.memset(t, 0.0))
            const(lambda e: e.affine_select(out=t, in_=t, compare_op=ALU.not_equal, fill=1.0, base=0,
                                            pattern=[[-1, n]], channel_multiplier=1))

        diagonal(ident[:, :])
        diagonal(ident_bf[:, :])

        mask_s = sb("mask_s", [P, P])
        const(lambda e: e.memset(mask_s[:, :], 0.0))
        const(lambda e: e.affine_select(out=mask_s[:, :], in_=mask_s[:, :], compare_op=ALU.is_ge, fill=NEG,
                                        base=0, pattern=[[-1, P]], channel_multiplier=1))
        before = sb("before", [P, P], BF16)
        const(lambda e: e.memset(before[:, :], 0.0))
        const(lambda e: e.affine_select(out=before[:, :], in_=before[:, :], compare_op=ALU.is_ge, fill=1.0,
                                        base=0, pattern=[[-1, P]], channel_multiplier=1))
        ones_bf = sb("ones_bf", [P, P], BF16)
        const(lambda e: e.memset(ones_bf[:, :], 1.0))
        zeros_bf = sb("zeros_bf", [P, QB], BF16)
        zeros_done = const(lambda e: e.memset(zeros_bf[:, :], 0.0))
        carry = sb("carry", [P, E, NT])
        const(lambda e: e.memset(carry[:, :, :], 1.0))
        const(lambda e: e.memset(carry[:, :, 0:1], 0.0))
        work = sb("work", [P, WORK])

        def iota(name, shape, pattern, mult=0, base=0, dt=F32):
            t = sb(name, shape, dt)
            ti = work[:, 0:shape[1]].bitcast(I32)
            const(lambda e: e.iota(ti, pattern=pattern, base=base, channel_multiplier=mult))
            const(lambda e: e.tensor_copy(t[:, :], ti))
            return t
        lo_ids = iota("lo_ids", [P, P], [[1, P]], dt=BF16)
        hi_ids = iota("hi_ids", [P, N_SUB], [[P, N_SUB]], dt=BF16)
        token_code_bits = sb("token_code_bits", [P, NT], I32)
        const(lambda e: e.iota(token_code_bits[:, :], pattern=[[P, NT]], base=CODE_0, channel_multiplier=1))
        const(lambda e: e.tensor_copy(work[:, 0:NT], token_code_bits[:, :]))
        const(lambda e: e.tensor_scalar(work[:, NT:2 * NT], work[:, 0:NT], 2.0 ** 16, None, ALU.mult))
        const(lambda e: e.tensor_copy(token_code_bits[:, :], work[:, NT:2 * NT]))
        token_code = token_code_bits[:, :].bitcast(F32)
        tile_steps = iota("tile_steps", [P, S // TILE], [[TILE, S // TILE]])
        tile_ids = iota("tile_ids", [P, N_TILES], [[1, N_TILES]])
        tile_col = iota("tile_col", [P, 1], [[0, 1]], mult=1)
        expert_ids = iota("expert_ids", [P, E], [[1, E]])
        expert_rank = iota("expert_rank", [P, E], [[-1, E]], base=E)
        ones_e = sb("ones_e", [P, E])
        const(lambda e: e.memset(ones_e[:, :], 1.0))
        consts_done = (s_const, s_const.count)

        GRP = 8
        x_loaded = []
        for g in range(NT // GRP):
            x_loaded.append(dma("sync", x_res[:, g * GRP:(g + 1) * GRP, :],
                                x_in.rearrange("(i p) d -> p i d", p=P)[:, g * GRP:(g + 1) * GRP, :],
                                [], sig(f"x_loaded{g}")))
        gate_w_sb = sb("gate_w_sb", [P, KD, E])
        gate_b_sb = sb("gate_b_sb", [P, E])
        s_small = sig("small_loads")
        dma("scalar", gate_w_sb[:, :, :], gate_w.rearrange("(k p) e -> p k e", p=P), [], s_small)
        small_loaded = dma("scalar", gate_b_sb[:, :], gate_b.partition_broadcast(P), [], s_small)
        s_attw = sig("attention_weights")
        dma("scalar", w_qkv_sb[:, :, :], w_qkv_t.rearrange("(k p) o -> p k o", p=P), [], s_attw)
        attw_loaded = dma("scalar", w_out_sb[:, :, :], w_out_t.rearrange("(k p) o -> p k o", p=P), [], s_attw)

        s_zero = sig("zero_rows_stored")
        for f in range(2):
            zero_stored = dma("scalar", table[f][0:1, :].rearrange("o (a b) -> (o a) b", a=2),
                              zeros_bf[:, :].bitcast(F32)[0:2, 0:ROW // 2], [zeros_done], s_zero)

        experts = phase[:, :].rearrange("p (e l w) -> p e l w", e=E, l=LAYERS)
        v_aug = phase[:, 0:NT * H * VW].rearrange("p (i h w) -> p i h w", i=NT, h=H)

        def load_experts(f, waits):
            s = sig(f"experts_loaded{f}")
            for l, w in enumerate((w1, w2, w3)):
                for k in range(KD):
                    m = dma("sync", experts[:, :, l, k * D:(k + 1) * D],
                            w.rearrange("e (k p) o -> p k e o", p=P)[:, k], waits, s)
            return dma("sync", experts[:, :, :, KD * D:WROW], bias_cols, waits, s)

        s_stat, s_eps, s_sqrt, s_rstd = sig("bn_stats"), sig("var_eps"), sig("sqrt"), sig("rstd")
        s_mv, s_norm, s_tr = sig("mean_var"), sig("normed"), sig("transposed")
        s_feat = sig("feat_copied")
        GROUPS = NT // GRP

        def layer_norm(before_it, consume):
            normed, spread = {}, {}

            def statistics(g):
                x_ready = before_it["add"](g)
                tiles = range(g * GRP, (g + 1) * GRP)
                for i in tiles:
                    st = put("vector", lambda e, i=i: e.bn_stats(stats[:, i, :], x_res[:, i, :]),
                             [x_ready[i - g * GRP]], s_stat)
                for i in tiles:
                    mv = put("vector", lambda e, i=i: e.bn_aggr(mean_var[:, i, :], stats[:, i, :]), [st], s_mv)
                a, b = g * GRP, (g + 1) * GRP
                ve = put("vector", lambda e: e.tensor_scalar(
                    rstd[:, 0, a:b], mean_var[:, a:b, 1], EPS, None, ALU.add), [mv], s_eps)
                spread[g] = ve

            def normalise(g):
                tiles = range(g * GRP, (g + 1) * GRP)
                a, b = g * GRP, (g + 1) * GRP
                sq = put("scalar", lambda e: e.activation(rstd[:, 1, a:b], rstd[:, 0, a:b], ACT.Sqrt),
                         [spread[g]], s_sqrt)
                rs = put("vector", lambda e: e.reciprocal(rstd[:, 0, a:b], rstd[:, 1, a:b]), [sq], s_rstd)
                for i in tiles:
                    normed[i] = put("vector", lambda e, i=i: e.tensor_scalar(
                        rows[:, i, 0:D], x_res[:, i, :], mean_var[:, i, 0:1], rstd[:, 0, i:i + 1],
                        ALU.subtract, ALU.mult), [rs, *before_it["rows"](g)], s_norm)

            def transpose(g):
                marks = []
                for i0 in range(g * GRP, (g + 1) * GRP, 4):
                    for k in range(KD):
                        bk = k
                        for i in range(i0, i0 + 4):
                            tr = put("tensor", lambda e, i=i, k=k, bk=bk, i0=i0: e.transpose(
                                bank[bk][:, (i - i0) * P:(i - i0 + 1) * P], rows[:, i, k * P:(k + 1) * P],
                                ident[:, :]), [normed[i], consts_done, *free[bk]], s_tr)
                        mk = put("scalar", lambda e, k=k, bk=bk, i0=i0: e.activation(
                            feat[:, k, i0 * P:(i0 + 4) * P], bank[bk][:, :], ACT.Copy),
                            [tr, *before_it["feat"](g)], s_feat)
                        free[bk] = (mk,)
                        marks.append(mk)
                return marks

            statistics(0)
            normalise(0)
            for g in range(GROUPS):
                if g + 1 < GROUPS:
                    statistics(g + 1)
                marks = transpose(g)
                if g + 1 < GROUPS:
                    normalise(g + 1)
                consume(g, marks)

        fat = [0]

        def fcarve(n):
            fat[0] += n
            return feat[:, 1, fat[0] - n:fat[0]]

        logits = fcarve(NT * E).rearrange("p (i e) -> p i e", e=E)
        probs = fcarve(NT * E).rearrange("p (i e) -> p i e", e=E)
        scratch = fcarve(4 * NT * E).rearrange("p (n i e) -> p n i e", n=4, e=E)
        sel = fcarve(TOP * NT * E).rearrange("p (n i e) -> p n i e", n=TOP, e=E)
        chosen = fcarve(NT * E).rearrange("p (i e) -> p i e", e=E)
        chosen_bf = sb("chosen_bf", [P, NT, E], BF16)
        small = sb("small", [P, 12, NT])
        per_expert = sb("per_expert", [P, 12, E])
        code = sb("code", [P, N_SUB])
        row_no_f = sb("row_no_f", [P, N_SUB])
        row_no = sb("row_no", [P, N_SUB], U32)
        steps_gt = fcarve(E * S // TILE).rearrange("p (e t) -> p e t", e=E)
        tile_cmp = fcarve(N_TILES * E).rearrange("p (j e) -> p j e", e=E)
        tile_mask = fcarve(N_TILES * E).rearrange("p (j e) -> p j e", e=E)
        tile_exp = sb("tile_exp", [P, N_TILES])
        tile_exp_i = sb("tile_exp_i", [P, N_TILES], I32)
        tile_hot = sb("tile_hot", [P, 3, E])
        v_part = sb("v_part", [P, KD, N_TILES])
        v_rows = sb("v_rows", [P, D])
        v_half = sb("v_half", [P, D])
        s_gate, s_dve, s_gexp, s_ared = sig("gate_mm"), sig("routing"), sig("gate_exp"), sig("all_reduce")
        s_cnt, s_inv, s_table = sig("count_mm"), sig("inverse_mm"), sig("table_stored")
        s_hot, s_hot_g = sig("one_hots"), sig("one_hots_by_gpsimd")
        s_cht, s_chc = sig("chosen_tr"), sig("chosen_copy")
        s_slot = [sig(f"slot_tile{i}") for i in range(3)]
        s_stage, s_xt, s_xtc, s_wb, s_wbt, s_wbc = (sig("staged"), sig("tile_tr"), sig("tile_copied"),
                                                     sig("weight_col"), sig("weight_tr"), sig("weight_row"))
        s_mm = [sig(f"layer_mm{l}") for l in range(LAYERS)]
        s_act_a, s_act_v = sig("relu_by_scalar"), sig("relu_by_vector")
        s_wy, s_vp = sig("weighted"), sig("v_partial")
        s_vt, s_vr, s_vm, s_vh, s_cmb, s_xadd = (sig("v_tr"), sig("v_rows"), sig("v_mm"), sig("v_half"),
                                                 sig("combine"), sig("x_added"))

        at = [0]

        def carve(n):
            at[0] += n
            assert at[0] <= WORK
            return work[:, at[0] - n:at[0]]

        NXG = 3
        W_RING = LAYERS + 1
        x_slot = carve(NXG * TS * ROW).rearrange("p (b u r) -> p b u r", b=NXG, u=TS)
        staged = carve(2 * LAYERS * WROW).rearrange("p (b l w) -> p b l w", b=2, l=LAYERS)
        acts = carve(3 * 2 * KD * TILE).rearrange("p (l b k s) -> p l b k s", l=3, b=2, k=KD)
        weighted = carve(2 * KD * TILE).rearrange("p (b m s) -> p b m s", b=2, m=KD)
        w_row = carve(W_RING * TILE).rearrange("p (b s) -> p b s", b=W_RING)
        w_wide = carve(2 * TS * P).rearrange("p (b u s) -> p b u s", b=2, u=TS)
        w_pick = carve(2 * TS * E).rearrange("p (b u e) -> p b u e", b=2, u=TS)
        w_col = carve(2 * TS).rearrange("p (b u) -> p b u", b=2)
        HOT_RING = 16
        hot_lo = work[:, 0:HOT_RING * P // 2].bitcast(BF16).rearrange("p (b s) -> p b s", b=HOT_RING)
        hot_hi = work[:, HOT_RING * P // 2:HOT_RING * (P + N_SUB) // 2].bitcast(BF16).rearrange(
            "p (b s) -> p b s", b=HOT_RING)

        def bc(ap, axis, shape):
            return ap.unsqueeze(axis).to_broadcast(shape)

        def moe(f, before_it, experts_loaded):
            PNE = [P, NT, E]
            work_free = before_it["work"]
            gate_bank = bank[2]
            gate_marks = {}

            def gate(g, feat_marks):
                for i in range(g * GRP, (g + 1) * GRP):
                    for k in range(KD):
                        gate_marks[g] = put("tensor", lambda e, i=i, k=k: e.matmul(
                            gate_bank[:, i * E:(i + 1) * E], feat[:, k, i * P:(i + 1) * P], gate_w_sb[:, k, :],
                            start=(k == 0), stop=(k == KD - 1)), [small_loaded, *feat_marks, *free[2]], s_gate)

            layer_norm(before_it, gate)
            g_mm = gate_marks[GROUPS - 1]
            v_last, inv_marks = [None], {}

            def v(emit, *waits):
                v_last[0] = put("vector", emit, [v_last[0], *waits], s_dve)
                return v_last[0]

            gate_v = gate_bank[:, 0:NT * E].rearrange("p (i e) -> p i e", e=E)
            v(lambda e: e.tensor_tensor(logits[:, :, :], gate_v, bc(gate_b_sb[:, :], 1, PNE), ALU.add), g_mm)
            free[2] = (v_last[0],)
            pe = lambda n: per_expert[:, n, :]
            m = v(lambda e: e.tensor_reduce(pe(0), logits[:, :, :].rearrange("p i e -> p e i"), AX_X, ALU.max))
            m = put("gpsimd", lambda e: e.partition_all_reduce(pe(1), pe(0), P, REDUCE.max), [m], s_ared)
            m = v(lambda e: e.tensor_tensor(logits[:, :, :], logits[:, :, :], bc(pe(1), 1, PNE), ALU.subtract), m)
            m = put("scalar", lambda e: e.activation(probs[:, :, :], logits[:, :, :], ACT.Exp), [m], s_gexp)
            m = v(lambda e: e.tensor_reduce(pe(2), probs[:, :, :].rearrange("p i e -> p e i"), AX_X, ALU.add), m)
            m = put("gpsimd", lambda e: e.partition_all_reduce(pe(3), pe(2), P, REDUCE.add), [m], s_ared)
            v(lambda e: e.reciprocal(pe(4), pe(3)), m)
            v(lambda e: e.tensor_tensor(probs[:, :, :], probs[:, :, :], bc(pe(4), 1, PNE), ALU.mult))

            left = probs
            for c in range(TOP):
                top, rank = small[:, 2 * c, :], small[:, 2 * c + 1, :]
                v(lambda e, left=left, top=top: e.tensor_reduce(top, left[:, :, :], AX_X, ALU.max))
                v(lambda e, left=left, top=top: e.tensor_tensor(scratch[:, 0], left[:, :, :], bc(top, 2, PNE),
                                                                ALU.is_equal))
                v(lambda e: e.tensor_tensor(scratch[:, 1], scratch[:, 0], bc(expert_rank[:, :], 1, PNE), ALU.mult),
                  consts_done)
                v(lambda e, rank=rank: e.tensor_reduce(rank, scratch[:, 1], AX_X, ALU.max))
                v(lambda e, c=c, rank=rank: e.tensor_tensor(sel[:, c], scratch[:, 1], bc(rank, 2, PNE), ALU.is_equal))
                if c == 0:
                    v(lambda e: e.scalar_tensor_tensor(scratch[:, 2], sel[:, 0], -4.0, probs[:, :, :],
                                                       ALU.mult, ALU.add))
                    left = scratch[:, 2]
            v(lambda e: e.tensor_tensor(chosen[:, :, :], sel[:, 0], sel[:, 1], ALU.add))
            cb = v(lambda e: e.tensor_copy(chosen_bf[:, :, :], chosen[:, :, :]))
            w_done = v(lambda e: e.tensor_tensor(rows[:, :, D:ROW], chosen[:, :, :], probs[:, :, :], ALU.mult))

            for g in range(NT // GRP):
                table_stored = dma("sync", table[f][1:S + 1, :].rearrange("(i p) r -> p i r", p=P)
                                   [:, g * GRP:(g + 1) * GRP, :], rows[:, g * GRP:(g + 1) * GRP, :], [w_done], s_table)

            flat = chosen_bf[:, :, :].rearrange("p i e -> p (i e)")
            put("tensor", lambda e: e.matmul(bank[5][:, 0:NT * E], before[:, :], flat, start=True, stop=True),
                [cb, *free[5]], s_cnt)
            cnt = put("tensor", lambda e: e.matmul(bank[6][:, 0:NT * E], ones_bf[:, :], flat, start=True,
                                                   stop=True), [*free[6]], s_cnt)
            for i0 in range(0, NT, 4):
                bk = (i0 // 4) % 2
                for i in range(i0, i0 + 4):
                    t = put("tensor", lambda e, i=i, i0=i0, bk=bk: e.transpose(
                        bank[bk][0:E, (i - i0) * P:(i - i0 + 1) * P], chosen[:, i, :], ident[:, :]),
                        [*free[bk]], s_cht)
                cp = put("scalar", lambda e, i0=i0, bk=bk: e.activation(
                    feat[0:E, 0, i0 * P:(i0 + 4) * P], bank[bk][0:E, :], ACT.Copy), [t, g_mm], s_chc)
                free[bk] = (cp,)
            chosen_t_done = cp

            em = scratch[:, 0].rearrange("p i e -> p (i e)").rearrange("p (e i) -> p e i", e=E)
            run = scratch[:, 1].rearrange("p i e -> p (i e)").rearrange("p (e i) -> p e i", e=E)
            prior = scratch[:, 2].rearrange("p i e -> p (i e)").rearrange("p (e i) -> p e i", e=E)
            v(lambda e: e.tensor_copy(em, bank[6][:, 0:NT * E].rearrange("p (i e) -> p e i", e=E)), cnt)
            free[6] = (v_last[0],)
            fl = lambda ap: ap.rearrange("p e i -> p (e i)")
            v(lambda e: e.tensor_tensor_scan(fl(run), fl(carry[:, :, :]), fl(em), 0.0, ALU.mult, ALU.add))
            v(lambda e: e.tensor_tensor(prior, run, em, ALU.subtract))
            SE = [P, E, S // TILE]
            v(lambda e: e.tensor_tensor(steps_gt[:, :, :], run[:, :, NT - 1:NT].to_broadcast(SE),
                                        bc(tile_steps[:, :], 1, SE), ALU.is_gt))
            v(lambda e: e.tensor_reduce(pe(5), steps_gt[:, :, :], AX_X, ALU.add))
            v(lambda e: e.tensor_tensor_scan(pe(6), ones_e[:, :], pe(5), 0.0, ALU.mult, ALU.add))
            v(lambda e: e.tensor_tensor(pe(7), pe(6), pe(5), ALU.subtract))
            v(lambda e: e.tensor_scalar(pe(8), pe(7), float(TILE), None, ALU.mult))
            v(lambda e: e.tensor_tensor(scratch[:, 3], bank[5][:, 0:NT * E].rearrange("p (i e) -> p i e", e=E),
                                        prior.rearrange("p e i -> p i e"), ALU.add))
            free[5] = (v_last[0],)
            v(lambda e: e.tensor_tensor(scratch[:, 3], scratch[:, 3], bc(pe(8), 1, PNE), ALU.add))
            for c in range(TOP):
                slot, hi, lo = small[:, 4 + 3 * c, :], small[:, 5 + 3 * c, :], small[:, 6 + 3 * c, :]
                v(lambda e, c=c: e.tensor_tensor(scratch[:, 0], sel[:, c], scratch[:, 3], ALU.mult))
                v(lambda e, slot=slot: e.tensor_reduce(slot, scratch[:, 0], AX_X, ALU.add))
                v(lambda e, slot=slot, lo=lo: e.tensor_scalar(lo, slot, 0.5 - P / 2, MAGIC, ALU.add, ALU.add))
                v(lambda e, hi=hi, lo=lo: e.tensor_scalar(hi, lo, MAGIC, None, ALU.subtract))
                digits = v(lambda e, slot=slot, hi=hi, lo=lo: e.tensor_tensor(lo, slot, hi, ALU.subtract))
                for i in range(NT):
                    col_lo, col_hi = small[:, 6 + 3 * c, i:i + 1], small[:, 5 + 3 * c, i:i + 1]
                    b = c * NT + i
                    waits = [digits, *work_free, inv_marks.get(b - HOT_RING)]
                    put("vector", lambda e, b=b, col=col_lo: e.tensor_scalar(
                        hot_lo[:, b % HOT_RING], lo_ids[:, :], col, None, ALU.is_equal), waits, s_hot)
                    engine, s_done = ("vector", s_hot) if i % 3 else ("gpsimd", s_hot_g)
                    put(engine, lambda e, b=b, col=col_hi, i=i: e.tensor_scalar(
                        hot_hi[:, b % HOT_RING], hi_ids[:, :], col, token_code[:, i:i + 1], ALU.is_equal, ALU.mult),
                        waits, s_done)
                    hot_v, hot_g = (s_hot, s_hot.count), (s_hot_g, s_hot_g.count)
                    inv_marks[b] = put("tensor", lambda e, b=b: e.matmul(
                        bank[7][:, 0:N_SUB], hot_lo[:, b % HOT_RING], hot_hi[:, b % HOT_RING],
                        start=(b == 0), stop=(b == TOP * NT - 1)), [hot_v, hot_g, *free[7]], s_inv)
            v(lambda e: e.tensor_copy(code[:, :], bank[7][:, 0:N_SUB]), inv_marks[TOP * NT - 1])
            free[7] = (v_last[0],)
            v(lambda e: e.tensor_copy(row_no_f[:, :], code[:, :].bitcast(I32)))
            v(lambda e: e.tensor_scalar(row_no_f[:, :], row_no_f[:, :], 2.0 ** -16, 1.0 - CODE_0, ALU.mult, ALU.add))
            v(lambda e: e.tensor_scalar(row_no_f[:, :], row_no_f[:, :], 0.0, None, ALU.max))
            row_no_done = v(lambda e: e.tensor_copy(row_no[:, :], row_no_f[:, :]))
            TE = [P, N_TILES, E]
            v(lambda e: e.tensor_tensor(tile_cmp[:, :, :], bc(tile_ids[:, :], 2, TE), bc(pe(6), 1, TE), ALU.is_ge))
            v(lambda e: e.tensor_reduce(tile_exp[:, :], tile_cmp[:, :, :], AX_X, ALU.add))
            v(lambda e: e.tensor_scalar(tile_exp[:, :], tile_exp[:, :], float(E - 1), None, ALU.min))
            tile_exp_done = v(lambda e: e.tensor_copy(tile_exp_i[:, :], tile_exp[:, :]))
            masks = v(lambda e: e.tensor_tensor(tile_mask[:, :, :], bc(tile_exp[:, :], 2, TE),
                                                bc(expert_ids[:, :], 1, TE), ALU.is_equal))
            v(lambda e: e.tensor_scalar(tile_hot[:, 0, :], pe(7), tile_col[:, 0:1], None, ALU.is_le))
            v(lambda e: e.tensor_scalar(tile_hot[:, 1, :], pe(6), tile_col[:, 0:1], None, ALU.is_le))
            hot = v(lambda e: e.tensor_tensor(tile_hot[:, 2, :], tile_hot[:, 0, :], tile_hot[:, 1, :], ALU.subtract))

            loaded, xt_done, xt_copied, w_ready = {}, {}, {}, {}
            stage_done = {(l, b): () for l in range(LAYERS) for b in range(2)}
            staged_marks, layer_marks, relu_marks = {}, {}, {}
            x_free = {}
            wy_marks, vp_marks, wide_read, widened = {}, {}, {}, {}
            work_free = [*work_free, inv_marks[TOP * NT - 1]]

            def stage(j, l):
                if not 0 <= j < N_TILES:
                    return

                def emit(e):
                    expert = e.value_load(tile_exp_i[0:1, j:j + 1], min_val=0, max_val=E - 1)
                    return e.tensor_copy(staged[:, j % 2, l, :],
                                         experts[:, bass.ds(expert, 1), l, :].rearrange("p a w -> p (a w)"))
                staged_marks[j, l] = put("vector", emit, [
                    tile_exp_done, experts_loaded, *work_free, layer_marks.get((j - 2, l)),
                    *relu_marks.get((j - 2, l), ())], s_stage)

            def load(j):
                if j >= N_TILES:
                    return
                for u in range(TS):
                    n = j * TS + u
                    loaded[j] = put("gpsimd", lambda e, u=u, n=n: e.indirect_dma_start(
                        out=x_slot[:, j % NXG, u, :], out_offset=None, in_=table[f],
                        in_offset=bass.IndirectOffsetOnAxis(ap=row_no[:, n:n + 1], axis=0)),
                        [row_no_done, zero_stored, table_stored, *x_free.get(j - NXG, ())], s_slot[j % NXG], 16)

            def widen_weight(j):
                if j >= N_TILES:
                    return
                b = j % 2
                pk = put("vector", lambda e: e.tensor_tensor(
                    w_pick[:, b], x_slot[:, j % NXG, :, D:ROW], bc(tile_mask[:, j, :], 1, [P, TS, E]), ALU.mult),
                    [loaded[j], masks, *work_free], s_wb)
                pk = put("vector", lambda e: e.tensor_reduce(w_col[:, b], w_pick[:, b], AX_X, ALU.add), [pk], s_wb)
                widened[j] = put("vector", lambda e: e.tensor_copy(w_wide[:, b], bc(w_col[:, b], 2, [P, TS, P])),
                                 [pk, wide_read.get(j - 2)], s_wb)

            def transpose_weight(j):
                if j >= N_TILES:
                    return
                for u in range(TS):
                    wt = put("tensor", lambda e, u=u: e.transpose(
                        bank[1][:, u * P:(u + 1) * P], w_wide[:, j % 2, u], ident[:, :]), [widened[j], *free[1]], s_wbt)
                wide_read[j] = wt
                w_ready[j] = put("scalar", lambda e: e.activation(w_row[:, j % W_RING], bank[1][:, 0:TILE], ACT.Copy),
                                 [wt, *wy_marks.get(j - W_RING, ()), *work_free], s_wbc)
                free[1] = (w_ready[j],)

            def transpose_tile(j):
                if j >= N_TILES:
                    return
                b = j % 2
                for u in range(TS):
                    for k in range(KD):
                        xt_done[j] = put("tensor", lambda e, u=u, k=k: e.transpose(
                            bank[0][:, k * TILE + u * P:k * TILE + (u + 1) * P],
                            x_slot[:, j % NXG, u, k * P:(k + 1) * P], ident[:, :]), [loaded[j], *free[0]], s_xt)
                x_free[j] = (xt_done[j], widened[j])
                xt_copied[j] = put("scalar", lambda e: e.activation(
                    acts[:, 0, b].rearrange("p k s -> p (k s)"), bank[0][:, :], ACT.Copy),
                    [xt_done[j], layer_marks.get((j - 2, 0)), *work_free], s_xtc)
                free[0] = (xt_copied[j],)

            def layer(j, l):
                if not 0 <= j < N_TILES:
                    return
                b = j % 2
                src = (xt_copied[j],) if l == 0 else relu_marks[j, l - 1]
                bk = 2 + l
                for m in range(KD):
                    for k in range(KD):
                        mm = put("tensor", lambda e, m=m, k=k: e.matmul(
                            bank[bk][:, m * TILE:(m + 1) * TILE],
                            staged[:, b, l, k * D + m * P:k * D + (m + 1) * P], acts[:, l, b, k],
                            start=(k == 0), stop=(k == KD - 1)),
                            [staged_marks[j, l], *src, *free[bk]], s_mm[l] if m == k == KD - 1 else None)
                layer_marks[j, l] = mm
                bias = lambda m: staged[:, b, l, KD * D + m:KD * D + m + 1]
                psum = lambda m: bank[bk][:, m * TILE:(m + 1) * TILE]
                if l < LAYERS - 1:
                    dst_free = layer_marks.get((j - 2, l + 1))
                    for m in range(KD):
                        if l == 0:
                            relu = put("scalar", lambda e, m=m: e.activation(
                                acts[:, l + 1, b, m], psum(m), ACT.Relu, bias=bias(m)), [mm, dst_free], s_act_a)
                        else:
                            relu = put("vector", lambda e, m=m: e.tensor_scalar(
                                acts[:, l + 1, b, m], psum(m), bias(m), 0.0, ALU.add, ALU.max), [mm, dst_free], s_act_v)
                    relu_marks[j, l] = (relu,)
                    free[bk] = (relu,)
                else:
                    for m in range(KD):
                        wy = put("vector", lambda e, m=m: e.scalar_tensor_tensor(
                            weighted[:, b, m], psum(m), bias(m), w_row[:, j % W_RING], ALU.add, ALU.mult),
                            [mm, w_ready[j], *vp_marks.get(j - 2, ())], s_wy)
                        vp = put("scalar", lambda e, m=m: e.activation(
                            weighted[:, b, m], weighted[:, b, m], ACT.Relu, accum_out=v_part[:, m, j:j + 1]),
                            [wy], s_vp)
                    free[bk] = (wy,)
                    relu_marks[j, l] = (wy,)
                    wy_marks[j] = (wy,)
                    vp_marks[j] = (vp,)

            load(0)
            load(1)
            stage(0, 0)
            for j in range(N_TILES + LAYERS):
                load(j + 2)
                widen_weight(j)
                layer(j - 3, 2)
                stage(j - 1, 2)
                transpose_tile(j)
                layer(j - 2, 1)
                stage(j, 1)
                transpose_weight(j)
                layer(j - 1, 0)
                stage(j + 1, 0)
            work_done = [layer_marks[N_TILES - 1, 2], *wy_marks[N_TILES - 1], *vp_marks[N_TILES - 1],
                         staged_marks[N_TILES - 1, LAYERS - 1]]

            for m in range(KD):
                t = put("tensor", lambda e, m=m: e.transpose(bank[5][0:N_TILES, m * P:(m + 1) * P],
                                                             v_part[:, m, :], ident[:, :]),
                        [*vp_marks[N_TILES - 1], *free[5]], s_vt)
            c = put("vector", lambda e: e.tensor_copy(v_rows[0:N_TILES, :], bank[5][0:N_TILES, 0:D]), [t], s_vr)
            free[5] = (c,)
            t = put("tensor", lambda e: e.matmul(bank[6][0:E, 0:D], tile_hot[0:N_TILES, 2, :], v_rows[0:N_TILES, :],
                                                 start=True, stop=True), [c, hot, *free[6]], s_vm)
            vh = put("vector", lambda e: e.tensor_scalar(v_half[0:E, :], bank[6][0:E, 0:D], 0.5, None, ALU.mult),
                     [t], s_vh)
            free[6] = (vh,)
            combined = {}

            def add(g):
                marks = []
                for i0 in range(g * GRP, (g + 1) * GRP, 2):
                    bk = 4 + (i0 // 2) % 2
                    for i in (i0, i0 + 1):
                        combined[g] = put("tensor", lambda e, i=i, i0=i0, bk=bk: e.matmul(
                            bank[bk][:, (i - i0) * D:(i - i0 + 1) * D], feat[0:E, 0, i * P:(i + 1) * P], v_half[0:E, :],
                            start=True, stop=True), [vh, chosen_t_done, *free[bk]], s_cmb)
                    xm = put("vector", lambda e, i0=i0, bk=bk: e.tensor_tensor(
                        x_res[:, i0:i0 + 2, :], x_res[:, i0:i0 + 2, :],
                        bank[bk][:, :].rearrange("p (a d) -> p a d", a=2), ALU.add), [combined[g]], s_xadd)
                    free[bk] = (xm,)
                    marks += [xm, xm]
                return marks

            return dict(add=add, work=work_done, rows=lambda g: [table_stored], feat=lambda g: [combined[g]],
                        phase=[staged_marks[N_TILES - 1, 2]])

        def attention(before_it):
            work_free, phase_free = before_it["work"], before_it["phase"]
            at[0] = 0
            bf = lambda ap: ap.bitcast(BF16)
            stack = bf(carve(2 * 2 * S // 2)).rearrange("p (b c s) -> p b c s", b=2, c=2)
            maxima = carve(2 * NJ * TPJ * (NJ + 1)).rearrange("p (b j i c) -> p b j i c", b=2, j=NJ, i=TPJ)
            neg_max = carve(4 * TPJ).rearrange("p (b i) -> p b i", b=4)
            max_parts = bf(carve(4 * TPJ * M_PARTS // 2)).rearrange("p (b i m) -> p b i m", b=4, i=TPJ)
            recip = carve(2 * TPJ).rearrange("p (b i) -> p b i", b=2)
            p_ring = feat[:, 0, :].rearrange("p (r s) -> p r s", r=P_RING)
            acc_sb = feat[:, 1, 0:2 * QB].rearrange("p (b s) -> p b s", b=2)
            head_sum = feat[:, 1, 2 * QB:2 * QB + 2 * TPJ * VW].rearrange("p (b i w) -> p b i w", b=2, i=TPJ)
            at_v = NT * H * VW
            split_bf = bf(phase[:, at_v:at_v + SPLIT_BF * 3 * QB // 2]).rearrange("p (b t s) -> p b t s", b=SPLIT_BF, t=3)
            at_v += SPLIT_BF * 3 * QB // 2
            split_f = phase[:, at_v:at_v + SPLIT_F * QB].rearrange("p (b s) -> p b s", b=SPLIT_F)
            heads = rows[:, :, 0:D]

            s_pm, s_p1, s_r1, s_p2, s_p3 = (sig("proj_mm"), sig("part1"), sig("rest1"), sig("part2"), sig("part3"))
            s_wr = [sig(f"parts_stored{i}") for i in range(SPLIT_BF)]
            parts_stored = {}
            store = {}
            p3m, begun, chunks = {}, [], [0]

            def project_chunk(ob, sc, banks, feat_marks=()):
                n = chunks[0]
                chunks[0] += 1
                bk, b = banks[n % len(banks)], n % SPLIT_BF
                for k in range(KD):
                    mm = put("tensor", lambda e, k=k: e.matmul(
                        bank[bk][:, :], w_qkv_sb[:, k, ob * P:(ob + 1) * P], feat[:, k, sc * QB:(sc + 1) * QB],
                        start=(k == 0), stop=(k == KD - 1)), [attw_loaded, *feat_marks, *free[bk]], s_pm)
                p1 = put("scalar", lambda e: e.activation(split_bf[:, b, 0], bank[bk][:, :], ACT.Copy),
                         [mm, store.get(n - SPLIT_BF), *phase_free], s_p1)
                free[bk] = None
                begun.append((n, ob, sc, bk, p1))

            def finish_chunk():
                n, ob, sc, bk, p1 = begun.pop(0)
                b, bf_ = n % SPLIT_BF, n % SPLIT_F
                r1 = put("vector", lambda e: e.tensor_tensor(split_f[:, bf_], bank[bk][:, :], split_bf[:, b, 0],
                                                             ALU.subtract),
                         [p1, p3m.get(n - SPLIT_F)], s_r1)
                free[bk] = (r1,)
                p2 = put("scalar", lambda e: e.activation(split_bf[:, b, 1], split_f[:, bf_], ACT.Copy), [r1], s_p2)
                p3m[n] = put("gpsimd", lambda e: e.tensor_tensor(split_bf[:, b, 2], split_f[:, bf_],
                                                                 split_bf[:, b, 1], ALU.subtract),
                             [p2, store.get(n - SPLIT_BF)], s_p3)
                qk, r0 = ob // KD, (ob % KD) * P
                store[n] = dma("sync", parts_dram[qk, :, r0:r0 + P, sc * QB:(sc + 1) * QB]
                               .rearrange("t r s -> r t s"), split_bf[:, b], [p3m[n], p1, p2], s_wr[b])
                parts_stored[ob] = tuple(store[m] for m in range(max(n + 1 - SPLIT_BF, 0), n + 1))

            s_vmm, s_vcp, s_ones = sig("value_mm"), sig("v_copied"), sig("ones_set")
            v_copied = [None]

            def project(g, feat_marks):
                for i in range(g * GRP, (g + 1) * GRP):
                    bk = 6 + i % 2
                    for k in range(KD):
                        mm = put("tensor", lambda e, k=k, i=i, bk=bk: e.matmul(
                            bank[bk][:, 0:D], feat[:, k, i * P:(i + 1) * P], w_qkv_sb[:, k, 2 * D:3 * D],
                            start=(k == 0), stop=(k == KD - 1)), [attw_loaded, *feat_marks, *free[bk]], s_vmm)
                    v_copied[0] = put("scalar", lambda e, i=i, bk=bk: e.activation(
                        v_aug[:, i, :, 0:HD], bank[bk][:, 0:D].rearrange("p (h d) -> p h d", h=H), ACT.Copy),
                        [mm, *phase_free], s_vcp)
                    free[bk] = (v_copied[0],)
                for sc in range(g * GRP // TPJ, (g + 1) * GRP // TPJ):
                    for ob in (0, KD):
                        project_chunk(ob, sc, (2, 3), feat_marks)
                        if len(begun) > 1:
                            finish_chunk()

            s_stack = [sig(f"stack{i}") for i in range(2)]
            stack_loaded = {}
            b_last = {}

            def load_stack(h):
                half = h // (H // KD)
                waits = [*parts_stored[half], *parts_stored[KD + half], *work_free,
                         b_last.get(h - 2)]
                r = 0
                for part, count in enumerate(K_PARTS):
                    q_rows = parts_dram[0, part, h * HD:(h + 1) * HD, :].unsqueeze(0).to_broadcast([count, HD, S])
                    k_rows = parts_dram[1, 0:count, h * HD:(h + 1) * HD, :]
                    for c, src in enumerate((q_rows, k_rows)):
                        stack_loaded[h] = dma("sync", stack[r * HD:(r + count) * HD, h % 2, c, :],
                                              src, waits, s_stack[h % 2])
                    r += count

            ones_set = put("gpsimd", lambda e: e.memset(v_aug[:, :, :, HD:VW], 1.0), [*phase_free], s_ones)
            for b in range(2):
                ones_set = put("gpsimd", lambda e, b=b: e.memset(
                    stack[QK_ROWS:QK_ROWS + M_PARTS, b, 1, :], 1.0), [*work_free, ones_set], s_ones)
            mx_set = put("gpsimd", lambda e: e.memset(maxima, NEG), [ones_set], s_ones)
            layer_norm(before_it, project)
            finish_chunk()
            load_stack(0)
            feat_read = [None]

            s_s, s_e, s_pv, s_acc, s_sum, s_rl, s_head = (sig("scores_t"), sig("exp"), sig("pv"), sig("acc_copied"),
                                                          sig("acc_transposed"), sig("recip"), sig("head_out"))
            s_a, s_mx, s_neg, s_mp, s_mt, s_mrow = (sig("scores"), sig("max_part"), sig("neg_max"),
                                                    sig("max_parts"), sig("max_tr"), sig("max_row"))
            put("tensor", lambda e: e.matmul(bank[ACC_BANK][:, :], zeros_bf[:, 0:P], zeros_bf[:, :], start=True,
                                             stop=True), [*free[ACC_BANK]], s_pv)

            units = [(h, j) for h in range(H) for j in range(NJ)]
            a_items = [(h, j, i, c) for h, j in units for i in range(TPJ) for c in range(j + 1)]
            b_items = [(h, j, t) for h, j in units for t in range(TPJ * (j + 1))]
            assert len(a_items) == len(b_items)
            mrow_done, neg_done, p_marks, exp_marks, pv_marks, mp_marks = {}, {}, {}, {}, {}, {}

            def a_item(n):
                h, j, i, c = a_items[n]
                bk = A_BANKS[n % len(A_BANKS)]
                w = QB if c < j else (i + 1) * P
                q0 = (TPJ * j + i) * P
                mm = put("tensor", lambda e: e.matmul(
                    bank[bk][:, 0:w], stack[0:QK_ROWS, h % 2, 0, q0:q0 + P], stack[0:QK_ROWS, h % 2, 1, c * QB:c * QB + w],
                    start=True, stop=True), [stack_loaded[h], *free[bk]], s_a)
                col = lambda k: maxima[:, h % 2, j, i, k:k + 1]
                last = None
                prev = neg_done.get((h - 2, j))
                full = w if c < j else w - P
                if full:
                    last = put("vector", lambda e: e.tensor_reduce(col(c if c < j else NJ), bank[bk][:, 0:full], AX_X, ALU.max),
                               [mm, mx_set, prev], s_mx)
                if c == j:
                    last = put("vector", lambda e: e.tensor_tensor_reduce(
                        bank[bk][:, w - P:w], bank[bk][:, w - P:w], mask_s[:, :], 1.0, NEG, ALU.add, ALU.max,
                        col(c)), [mm, mx_set, prev, consts_done], s_mx)
                free[bk] = (last,)
                if i == TPJ - 1 and c == j:
                    u = h * NJ + j
                    neg_done[h, j] = put("vector", lambda e: e.tensor_reduce(
                        neg_max[:, u % 4, :], maxima[:, h % 2, j], AX_X, ALU.max, negate=True),
                        [last, mp_marks.get(u - 4)], s_neg)
                    m1 = put("gpsimd", lambda e: e.tensor_copy(max_parts[:, u % 4, :, 0], neg_max[:, u % 4, :]),
                             [neg_done[h, j], mt_marks.get(u - 4)], s_mp)
                    mp_marks[u] = put("gpsimd", lambda e: e.tensor_tensor(
                        max_parts[:, u % 4, :, 1], neg_max[:, u % 4, :], max_parts[:, u % 4, :, 0], ALU.subtract),
                        [m1], s_mp)
                    return u
                return None

            mt_marks = {}

            def max_row(u):
                h, j = units[u]
                for i in range(TPJ):
                    mt_marks[u] = put("tensor", lambda e, i=i: e.matmul(
                        bank[M_BANK][QK_ROWS:QK_ROWS + M_PARTS, i * P:(i + 1) * P], max_parts[:, u % 4, i, :],
                        ident_bf[:, :], start=True, stop=True), [mp_marks[u], *free[M_BANK]], s_mt)
                mrow_done[u] = put("scalar", lambda e: e.activation(
                    stack[QK_ROWS:QK_ROWS + M_PARTS, h % 2, 0, j * QB:(j + 1) * QB],
                    bank[M_BANK][QK_ROWS:QK_ROWS + M_PARTS, :], ACT.Copy), [mt_marks[u], b_last.get(h - 2)], s_mrow)
                free[M_BANK] = (mrow_done[u],)

            def b_item(n):
                h, j, t = b_items[n]
                u = h * NJ + j
                bk = S_BANKS[n % len(S_BANKS)]
                diag = t - TPJ * j
                lo = max(diag, 0) * P
                mm = put("tensor", lambda e: e.matmul(
                    bank[bk][:, lo:QB], stack[0:QK_ROWS + M_PARTS, h % 2, 1, t * P:(t + 1) * P],
                    stack[0:QK_ROWS + M_PARTS, h % 2, 0, j * QB + lo:(j + 1) * QB], start=True, stop=True),
                    [mrow_done[u], stack_loaded[h], ones_set, *free[bk]], s_s)
                b_last[h] = mm
                exp_marks[n] = put("scalar", lambda e: e.activation(
                    p_ring[:, n % P_RING, lo:QB], bank[bk][:, lo:QB], ACT.Exp, scale=HD ** -0.5),
                    [mm, pv_marks.get(n - P_RING), feat_read[0]], s_e)
                free[bk] = (exp_marks[n],)
                if diag >= 0:
                    exp_marks[n] = put("gpsimd", lambda e: e.affine_select(
                        out=p_ring[:, n % P_RING, lo:lo + P], in_=p_ring[:, n % P_RING, lo:lo + P],
                        compare_op=ALU.is_ge, fill=0.0, base=0, pattern=[[1, P]], channel_multiplier=-1),
                        [exp_marks[n]], s_causal)

            def pv_group(n0, half):
                h, j, t0 = b_items[n0]
                u = h * NJ + j
                first = t0 == 0
                zero_start = first and j == 0
                if zero_start and half == 0:
                    for c in range(TPJ):
                        put("tensor", lambda e, c=c: e.matmul(
                            bank[ACC_BANK][32 * c:32 * c + VW, :], zeros_bf[:, 0:VW], zeros_bf[:, :],
                            start=True, stop=False), [*free[ACC_BANK]], s_pv)
                for c in range(TPJ):
                    t = t0 + c
                    lo, hi = max((t - TPJ * j) * P, half * QB // 2), (half + 1) * QB // 2
                    if lo >= hi:
                        continue
                    mark = put("tensor", lambda e, c=c, t=t, lo=lo, hi=hi: e.matmul(
                        bank[ACC_BANK][32 * c:32 * c + VW, lo:hi], v_aug[:, t, h, :], p_ring[:, (n0 + c) % P_RING, lo:hi],
                        start=(first and not zero_start and half == 0), stop=(t0 == TPJ * j and half == 1)),
                        [exp_marks[n0 + c], v_copied[0], ones_set, *free[ACC_BANK]], s_pv)
                    if half:
                        pv_marks[n0 + c] = mark
                if t0 == TPJ * j and half:
                    cp = put("scalar", lambda e: e.activation(acc_sb[:, u % 2, :], bank[ACC_BANK][:, :], ACT.Copy),
                             [pv_marks[n0 + TPJ - 1], sum_marks.get(u - 2), feat_read[0]], s_acc)
                    free[ACC_BANK] = (cp,)
                    return u, cp
                return None

            sum_marks = {}
            s_causal = sig("causal_zeros")
            s_hs = sig("head_sum")
            head_marks = []

            def finish_unit(u, cp):
                h, j = units[u]
                for i in range(TPJ):
                    sum_marks[u] = put("tensor", lambda e, i=i: e.transpose(
                        bank[O_BANK][:, i * P:(i + 1) * P], acc_sb[:, u % 2, i * P:(i + 1) * P], ident[:, :]),
                        [cp, *free[O_BANK]], s_sum)
                o = bank[O_BANK][:, :].rearrange("p (i c w) -> p i w c", i=TPJ, c=TPJ)
                hs = put("vector", lambda e: e.tensor_reduce(head_sum[:, u % 2], o[:, :, 0:VW, :], AX_X, ALU.add),
                         [sum_marks[u], head_marks[-2] if u >= 2 else None], s_hs)
                free[O_BANK] = (hs,)
                rl = put("vector", lambda e: e.reciprocal(recip[:, u % 2, :], head_sum[:, u % 2, :, HD]), [hs], s_rl)
                hm = put("vector", lambda e: e.tensor_tensor(
                    heads[:, TPJ * j:TPJ * (j + 1), h * HD:(h + 1) * HD], head_sum[:, u % 2, :, 0:HD],
                    bc(recip[:, u % 2, :], 2, [P, TPJ, HD]), ALU.mult), [rl], s_head)
                head_marks.append(hm)

            CHUNK_EVERY = 4
            rest = [(ob, sc) for ob in (1, KD + 1) for sc in range(NJ)]
            for _ in range(6):
                project_chunk(*rest.pop(0), S_BANKS)
                if len(begun) > 1:
                    finish_chunk()
            finish_chunk()
            assert len(rest) * CHUNK_EVERY <= LEAD
            MAX_LAG = 5
            due = {}
            total = len(a_items)
            unfinished = []
            for n in range(total + LEAD):
                if n % CHUNK_EVERY == 0 and rest:
                    project_chunk(*rest.pop(0), S_BANKS)
                    feat_read[0] = (s_pm, s_pm.count)
                if n % CHUNK_EVERY == 2 and begun:
                    finish_chunk()
                if n == LEAD:
                    load_stack(1)
                if n < total:
                    u = a_item(n)
                    if u is not None:
                        due.setdefault(n + MAX_LAG, []).append(u)
                for u in due.pop(n, []):
                    max_row(u)
                bn = n - LEAD
                if bn >= 0:
                    h, j, t = b_items[bn]
                    if j == 2 and t == 0 and 1 <= h < H - 1:
                        load_stack(h + 1)
                    b_item(bn)
                    group = bn - bn % TPJ
                    if bn % TPJ == 1 and group:
                        pv_group(group - TPJ, 0)
                    if bn % TPJ == 2 and unfinished:
                        finish_unit(*unfinished.pop())
                    if bn % TPJ == 3 and group:
                        done = pv_group(group - TPJ, 1)
                        if done:
                            unfinished.append(done)
            for u, cp in unfinished:
                finish_unit(u, cp)
            pv_group(total - TPJ, 0)
            finish_unit(*pv_group(total - TPJ, 1))
            all_heads = head_marks[-1]
            last_pv = pv_marks[total - 1]

            s_ht, s_hc, s_om, s_xo = sig("heads_tr"), sig("heads_copied"), sig("out_mm"), sig("x_attended")
            heads_read, projected, heads_copied = {}, {}, {}
            H_BANKS = (3, 6, 7)

            def transpose_heads(n):
                for k in range(KD):
                    bk = H_BANKS[(n * KD + k) % len(H_BANKS)]
                    for i in range(4 * n, 4 * n + 4):
                        tr = put("tensor", lambda e, i=i, k=k, bk=bk: e.transpose(
                            bank[bk][:, (i - 4 * n) * P:(i - 4 * n + 1) * P], rows[:, i, k * P:(k + 1) * P],
                            ident[:, :]), [all_heads, *free[bk]], s_ht)
                    cp = put("scalar", lambda e, k=k, bk=bk: e.activation(
                        feat[:, k, 4 * n * P:4 * (n + 1) * P], bank[bk][:, :], ACT.Copy),
                        [tr, last_pv, sum_marks[len(units) - 1]], s_hc)
                    free[bk] = (cp,)
                heads_read[4 * n // GRP] = tr
                heads_copied[n] = cp

            def add(g):
                marks = []
                for i0 in range(g * GRP, (g + 1) * GRP, 4):
                    if i0 == 0:
                        transpose_heads(0)
                    if i0 + 4 < NT:
                        transpose_heads(i0 // 4 + 1)
                    for i2 in range(i0, i0 + 4, 2):
                        bk = 4 + (i2 // 2) % 2
                        for i in (i2, i2 + 1):
                            for k in range(KD):
                                projected[g] = put("tensor", lambda e, i=i, i2=i2, k=k, bk=bk: e.matmul(
                                    bank[bk][:, (i - i2) * D:(i - i2 + 1) * D], feat[:, k, i * P:(i + 1) * P],
                                    w_out_sb[:, k, :], start=(k == 0), stop=(k == KD - 1)),
                                    [heads_copied[i0 // 4], *free[bk]], s_om)
                        xm = put("vector", lambda e, i2=i2, bk=bk: e.tensor_tensor(
                            x_res[:, i2:i2 + 2, :], x_res[:, i2:i2 + 2, :],
                            bank[bk][:, :].rearrange("p (a d) -> p a d", a=2), ALU.add), [projected[g]], s_xo)
                        free[bk] = (xm,)
                        marks += [xm, xm]
                return marks

            return dict(add=add, work=[last_pv], phase=[last_pv], rows=lambda g: [heads_read[g]],
                        feat=lambda g: [projected[g]])

        experts0 = load_experts(0, [])
        given = dict(add=lambda g: [x_loaded[g]] * GRP, work=[], phase=[], rows=lambda g: [], feat=lambda g: [])
        r = moe(0, given, experts0)
        r = attention(r)
        experts1 = load_experts(1, r["phase"])
        r = moe(1, r, experts1)
        s_out = sig("stored")
        out_t = out.rearrange("(i p) d -> p i d", p=P)
        for g in range(GROUPS):
            stored = dma("sync", out_t[:, g * GRP:(g + 1) * GRP, :], x_res[:, g * GRP:(g + 1) * GRP, :],
                         [r["add"](g)[-1]], s_out)
        q.lists["sync"].append(((stored,), lambda e: e.nop(), None, 0))

        block = ctx.enter_context(nc.Block())

        @block.sync
        def _(eng):
            q.run("sync", eng)

        @block.gpsimd
        def _(eng):
            q.run("gpsimd", eng)

        @block.scalar
        def _(eng):
            q.run("scalar", eng)

        @block.tensor
        def _(eng):
            q.run("tensor", eng)

        @block.vector
        def _(eng):
            q.run("vector", eng)


def kernel(**inputs):
    import numpy as np
    import concourse.bacc as bacc
    from concourse.bass_utils import run_bass_kernel_spmd

    given = {name: np.asarray(a) for name, a in inputs.items()}
    arrays = {
        "x": given["L0_attn_x"].reshape(S, D),
        "w_qkv_t": given["L0_attn_w_qkv"].T,
        "w_out_t": given["L0_attn_w_out"].T,
    }
    for name in ("gate_w", "gate_b", "w1", "w2", "w3"):
        arrays[name] = given["L0_ffn_" + name]
    biases = np.stack([given["L0_ffn_" + name] for name in ("b1", "b2", "b3")], axis=1)
    arrays["bias_cols"] = biases.reshape(E, LAYERS, KD, P).transpose(3, 0, 1, 2)
    arrays = {name: np.ascontiguousarray(a) for name, a in arrays.items()}
    nc = bacc.Bacc("TRN2", target_bir_lowering=False, num_devices=1)
    args = [nc.dram_tensor("in_" + name, a.shape, F32, kind="ExternalInput").ap() for name, a in arrays.items()]
    out = nc.dram_tensor("out", (S, D), F32, kind="ExternalOutput").ap()
    macaron_block(nc, *args, out)
    r = run_bass_kernel_spmd(nc, [{"in_" + name: a for name, a in arrays.items()}], core_ids=[0])
    return r.results[0]["out"].reshape(1, S, D)
```
